# Optimizing a Trainium2 kernel written in Bass

```python
import numpy as np
import jax
import jax.numpy as jnp

def _softmax(x, axis=-1):
    return jax.nn.softmax(x, axis=axis)

def _gelu(x):
    return jax.nn.gelu(x, approximate=True)

def _silu(x):
    return jax.nn.silu(x)

def _sigmoid(x):
    return jax.nn.sigmoid(x)

def _layernorm(x, axis=-1, eps=1e-05):
    m = jnp.mean(x, axis=axis, keepdims=True)
    v = jnp.var(x, axis=axis, keepdims=True)
    return (x - m) / jnp.sqrt(v + eps)

def _scatter_add(tgt, idx, src, axis=0):
    return tgt.at[idx].add(src)

def _segment_sum(src, seg, n):
    return jax.ops.segment_sum(src, seg, n)
kernel_name = 'mk_adaln_ffn_d1_seqx_r4_8de613'

def setup_inputs(seed: int=0):
    np.random.seed(seed)
    _w = jnp.asarray

    def _rec_inputs():
        import jax
        import jax.numpy as jnp
        _rk = jax.random.key(seed)
        x = 7.22e-05 + 1 * jax.random.normal(jax.random.fold_in(_rk, 1), (16, 256, 256), jnp.float32)
        _lenS = 256 - jax.random.randint(jax.random.fold_in(_rk, 7), (16,), 0, max(1, 256 // 4) + 1, jnp.int32)
        _lenS2 = 256 - jax.random.randint(jax.random.fold_in(_rk, 8), (16,), 0, max(1, 256 // 4) + 1, jnp.int32)
        fside_BxSxS_0 = 4.13588e-05 + 0.999923 * jax.random.normal(jax.random.fold_in(_rk, 11), (16, 256, 256), jnp.float32)
        itok_B_0_5 = jax.random.randint(jax.random.fold_in(_rk, 12), (16,), 0, 6, jnp.int32)
        return (x, fside_BxSxS_0, itok_B_0_5)
    x, fside_BxSxS_0, itok_B_0_5 = _rec_inputs()

    def _L0_cond_setup():
        import jax, jax.numpy as jnp
        import numpy as np
        B, S, D = (8, 256, 256)
        NUM_STAGES = 6
        key = jax.random.key(seed)
        k1, k2, k3, k4, k5 = jax.random.split(key, 5)
        return {'query': jax.random.normal(k1, (B, S, D), dtype=jnp.float32), 'key': jax.random.normal(k2, (B, S, D), dtype=jnp.float32), 'value': jax.random.normal(k3, (B, S, D), dtype=jnp.float32), 'braak_embed': jax.random.normal(k4, (NUM_STAGES, D), dtype=jnp.float32), 'braak_stages': jax.random.randint(k5, (B,), 0, NUM_STAGES, dtype=jnp.int64)}
    _L0_cond_all = _L0_cond_setup()
    _L0_cond_in = {k: v for k, v in _L0_cond_all.items() if k in ('braak_embed',)}
    del _L0_cond_all

    def _L0_ffn_setup():
        import jax, jax.numpy as jnp
        import numpy as np
        IN_FEATURES = 256
        ACT_BITS = 4

        def _hadamard(size: int) -> np.ndarray:
            h = np.array([[1.0]], dtype=np.float64)
            while h.shape[0] < size:
                h = np.block([[h, h], [h, -h]])
            return (h / np.sqrt(size)).astype(np.float32)

        def _quantize_activations(x, bits=ACT_BITS):
            pos = 2 ** (bits - 1) - 1
            neg = 2 ** (bits - 1)
            scale = jnp.clip(jnp.max(jnp.abs(jax.lax.stop_gradient(x)), axis=-1, keepdims=True), 1e-05) / pos
            q = jnp.clip(jnp.round(x / scale), -neg, pos) * scale
            return x + jax.lax.stop_gradient(q - x)

        def _ternary_quantize_ste(w):
            scale = jnp.clip(jnp.mean(jnp.abs(jax.lax.stop_gradient(w)), axis=1, keepdims=True), 1e-05)
            n = w / scale
            tern = jnp.where(n > 0.5, 1.0, jnp.where(n < -0.5, -1.0, 0.0))
            q = tern * scale
            return w + jax.lax.stop_gradient(q - w)
        key = jax.random.key(seed)
        k1, k2 = jax.random.split(key)
        x = jax.random.normal(k1, (8, 2048, IN_FEATURES), dtype=jnp.float32)
        bound = 1.0 / np.sqrt(IN_FEATURES)
        weight = jax.random.uniform(k2, (256, IN_FEATURES), dtype=jnp.float32, minval=-bound, maxval=bound)
        return {'x': x, 'weight': weight}
    _L0_ffn_all = _L0_ffn_setup()
    _L0_ffn_in = {k: v for k, v in _L0_ffn_all.items() if k in ('weight',)}
    del _L0_ffn_all
    return {'x': x, 'fside_BxSxS_0': fside_BxSxS_0, 'itok_B_0_5': itok_B_0_5, 'L0_cond_braak_embed': _L0_cond_in['braak_embed'], 'L0_ffn_weight': _L0_ffn_in['weight']}

def reference(x, fside_BxSxS_0, itok_B_0_5, L0_cond_braak_embed, L0_ffn_weight):
    import jax
    import jax.numpy as jnp

    def _L0_cond_ref(query, key, value, braak_embed, braak_stages):
        import jax, jax.numpy as jnp
        import numpy as np
        B, S, D = (8, 256, 256)
        NUM_STAGES = 6
        bias = braak_embed[braak_stages][..., None]
        q = query + bias
        attn = jnp.einsum('bsd,btd->bst', q, key)
        attn = jax.nn.softmax(attn, axis=-1)
        return jnp.einsum('bst,btd->bsd', attn, value)

    def _L0_ffn_ref(x, weight):
        import jax, jax.numpy as jnp
        import numpy as np
        IN_FEATURES = 256
        ACT_BITS = 4

        def _hadamard(size: int) -> np.ndarray:
            h = np.array([[1.0]], dtype=np.float64)
            while h.shape[0] < size:
                h = np.block([[h, h], [h, -h]])
            return (h / np.sqrt(size)).astype(np.float32)

        def _quantize_activations(x, bits=ACT_BITS):
            pos = 2 ** (bits - 1) - 1
            neg = 2 ** (bits - 1)
            scale = jnp.clip(jnp.max(jnp.abs(jax.lax.stop_gradient(x)), axis=-1, keepdims=True), 1e-05) / pos
            q = jnp.clip(jnp.round(x / scale), -neg, pos) * scale
            return x + jax.lax.stop_gradient(q - x)

        def _ternary_quantize_ste(w):
            scale = jnp.clip(jnp.mean(jnp.abs(jax.lax.stop_gradient(w)), axis=1, keepdims=True), 1e-05)
            n = w / scale
            tern = jnp.where(n > 0.5, 1.0, jnp.where(n < -0.5, -1.0, 0.0))
            q = tern * scale
            return w + jax.lax.stop_gradient(q - w)
        H = jnp.asarray(_hadamard(IN_FEATURES))
        xh = x @ H
        xq = _quantize_activations(xh)
        wq = _ternary_quantize_ste(weight)
        return jnp.einsum('bsi,oi->bso', xq, wq)
    x = x + _L0_ffn_ref(_L0_cond_ref(x, fside_BxSxS_0, fside_BxSxS_0, L0_cond_braak_embed, itok_B_0_5), L0_ffn_weight)
    return x

_drawn_inputs = setup_inputs


def setup_inputs(seed=0):
    import zlib

    import numpy as np

    out = dict(_drawn_inputs(seed))
    spreads = {}
    factors = {}
    for name, (base, spread) in spreads.items():
        noise = np.random.default_rng([zlib.crc32(name.encode()), seed]).standard_normal(out[name].shape)
        drawn = base * np.exp(spread * noise) if base else spread * noise
        out[name] = jnp.asarray(drawn.astype(out[name].dtype))
    for name, factor in factors.items():
        out[name] = (out[name] * factor).astype(out[name].dtype)
    return out
```

```python
from contextlib import ExitStack

import numpy as np

import concourse.bass as bass
from concourse import mybir

F32 = mybir.dt.float32
F32R = mybir.dt.float32r
BF16 = mybir.dt.bfloat16
I32 = mybir.dt.int32
ALU = mybir.AluOpType
ACT = mybir.ActivationFunctionType
AX = mybir.AxisListType

P = 128

POS = 7.0
MIN_ABS = 1e-5

CODE_BITS = 0x4040
CODE_ONE = 3.0
CODE_STEP = 64.0
MAGIC = float(3 * 2**22 + CODE_BITS)

LAG_LOAD_TURN = 0
LAG_SCORE = 1
LAG_MIX = 2
LAG_QUANT = 3
LAG_OUT = 4


def adaln_ffn_kernel(nc, x, f, itok, embed, weight, identity, hadamard, out):
    B, S, D = x.shape
    STAGES = embed.shape[0]
    O = weight.shape[0]
    T = S // P
    C = D // P
    W = T * D
    assert S % P == 0 and D % P == 0 and O == D == S and W == 512 and B % 2 == 0 and B >= 8

    x_dram = x.rearrange("b (p t) d -> b p (t d)", t=T)
    f_dram = f.rearrange("b (p t) d -> b p (t d)", t=T)
    out_dram = out.rearrange("b (p t) d -> b p (t d)", t=T)
    weight_dram = weight.rearrange("(t p) d -> p t d", p=P)
    hadamard_dram = hadamard.rearrange("(c p) d -> p c d", p=P)

    with ExitStack() as ctx:
        def sb(name, shape, dtype):
            return ctx.enter_context(nc.sbuf_tensor(name, shape, dtype))

        def bank(name, shape, dtype):
            return ctx.enter_context(nc.psum_tensor(name, shape, dtype))

        def sem(name):
            return ctx.enter_context(nc.semaphore(name))

        ident = sb("ident", [P, P], F32)
        ident16 = sb("ident16", [P, P], BF16)
        ones = sb("ones", [P, P], F32)
        had_raw = sb("had_raw", [P, C, D], F32)
        had = sb("had", [P, C, D], F32R)
        w_raw = sb("w_raw", [P, T, D], F32)
        w_scale = sb("w_scale", [P, T], F32)
        w_above = sb("w_above", [P, T], F32)
        w_below = sb("w_below", [P, T], F32)
        w_neg = sb("w_neg", [P, T, D], F32)
        tern = sb("tern", [P, T, D], BF16)
        tern_t = sb("tern_t", [P, C, O], BF16)
        w_diag = sb("w_diag", [P, T, P], F32)
        w_scale_row = sb("w_scale_row", [P, O], F32)
        stage_of = sb("stage_of", [STAGES, B], I32)
        stage_id = sb("stage_id", [STAGES, 1], F32)
        one_hot = sb("one_hot", [STAGES, B], F32)
        embed_sb = sb("embed_sb", [STAGES, S], F32)
        bias = sb("bias", [P, B, T], F32)

        x_all = sb("x_all", [P, B, W], F32)
        f_nat = sb("f_nat", [P, 2, T, D], F32)
        q_nat = sb("q_nat", [P, 2, T, D], F32)
        f_hi = sb("f_hi", [P, 2, C, S], F32R)
        f_lo = sb("f_lo", [P, 2, C, S], F32R)
        q_hi = sb("q_hi", [P, 2, C, S], F32R)
        q_lo = sb("q_lo", [P, 2, C, S], F32R)
        fh_hi = sb("fh_hi", [P, 2, T, D], F32R)
        fh_lo = sb("fh_lo", [P, 2, T, D], F32R)
        neg_max = sb("neg_max", [P, 2, T], F32)
        prob = sb("prob", [P, T, S], F32)
        prob_hi = sb("prob_hi", [P, C, S], F32R)
        prob_lo = sb("prob_lo", [P, C, S], F32R)
        row_sum = sb("row_sum", [P, 2, T], F32)
        inv_sum = sb("inv_sum", [P, 2, T], F32)
        least_scale = sb("least_scale", [P, 2, T], F32)
        abs_max = sb("abs_max", [P, T], F32)
        raw_scale = sb("raw_scale", [P, T], F32)
        inv_scale = sb("inv_scale", [P, 2, T], F32)
        out_scale = sb("out_scale", [P, 2, T], F32)
        code = sb("code", [P, T, D], F32)
        code_t = sb("code_t", [P, 2, C, S], BF16)
        scaled = sb("scaled", [P, 2, T, O], F32)
        result = sb("result", [P, 2, W], F32)

        f_bank = bank("f_bank", [P, C, S], F32)
        q_bank = bank("q_bank", [P, C, S], F32)
        score_bank = bank("score_bank", [P, T, S], F32)
        fh_bank = bank("fh_bank", [P, T, D], F32)
        prob_bank = bank("prob_bank", [P, C, S], F32)
        xh_bank = bank("xh_bank", [P, T, D], F32)
        code_bank = bank("code_bank", [P, 2 * C, S], BF16)
        out_bank = bank("out_bank", [P, T, O], F32)

        ident_loaded = sem("ident_loaded")
        had_loaded = sem("had_loaded")
        weight_loaded = sem("weight_loaded")
        bias_loaded = sem("bias_loaded")
        x_loaded = [sem(f"x_loaded{k}") for k in range(2)]
        f_loaded = [sem(f"f_loaded{k}") for k in range(2)]
        stored = [sem(f"stored{k}") for k in range(2)]
        ids_ready = sem("ids_ready")
        one_hot_ready = sem("one_hot_ready")
        bias_in_bank = sem("bias_in_bank")
        bias_ready = sem("bias_ready")
        ones_ready = sem("ones_ready")
        ident16_ready = sem("ident16_ready")
        had_ready = sem("had_ready")
        w_step = sem("w_step")
        tern_ready = sem("tern_ready")
        tern_in_bank = sem("tern_in_bank")
        tern_t_ready = sem("tern_t_ready")
        diag_ready = sem("diag_ready")
        row_in_bank = sem("row_in_bank")
        row_ready = sem("row_ready")

        q_ready = sem("q_ready")
        f_in_bank = sem("f_in_bank")
        q_in_bank = sem("q_in_bank")
        f_hi_ready = sem("f_hi_ready")
        f_lo_ready = sem("f_lo_ready")
        q_hi_ready = sem("q_hi_ready")
        q_lo_ready = sem("q_lo_ready")
        score_in_bank = sem("score_in_bank")
        neg_max_ready = sem("neg_max_ready")
        prob_ready = sem("prob_ready")
        sums_ready = sem("sums_ready")
        fh_in_bank = sem("fh_in_bank")
        fh_hi_ready = sem("fh_hi_ready")
        fh_lo_ready = sem("fh_lo_ready")
        prob_in_bank = sem("prob_in_bank")
        prob_hi_ready = sem("prob_hi_ready")
        prob_lo_ready = sem("prob_lo_ready")
        xh_in_bank = sem("xh_in_bank")
        abs_max_ready = sem("abs_max_ready")
        raw_scale_ready = sem("raw_scale_ready")
        inv_scale_ready = sem("inv_scale_ready")
        out_scale_ready = sem("out_scale_ready")
        code_ready = sem("code_ready")
        code_in_bank = sem("code_in_bank")
        code_t_ready = sem("code_t_ready")
        out_in_bank = sem("out_in_bank")
        scaled_ready = sem("scaled_ready")
        result_ready = sem("result_ready")

        block = ctx.enter_context(nc.Block())

        class Batch:

            def __init__(self, half, odd):
                self.half, self.k = half + odd // 2, odd % 2
                self.at = 2 * self.half + self.k

        LOOP_FROM = LAG_OUT // 2 + 1

        def peeled(i):
            return lambda lag: Batch(0, i - lag) if 0 <= i - lag < B else None

        def looped(half, odd):
            return lambda lag: Batch(half, odd - lag)

        def wait(engine, semaphore, count):
            if not (isinstance(count, int) and count <= 0):
                engine.wait_ge(semaphore, count)

        @block.sync
        def _(sp):
            sp.dma_start(ident[:, :], identity).then_inc(ident_loaded, 16)
            sp.dma_start(embed_sb[:, :], embed).then_inc(bias_loaded, 16)
            sp.dma_start(stage_of[:, :], itok.partition_broadcast(STAGES)).then_inc(bias_loaded, 16)

            def step(batch):
                if b := batch(-2):
                    wait(sp, f_in_bank, b.at - 1)
                    sp.dma_start(f_nat[:, b.k], f_dram[b.at]).then_inc(f_loaded[b.k], 16)
                    wait(sp, q_ready, b.at - 1)
                    sp.dma_start(x_all[:, b.at], x_dram[b.at]).then_inc(x_loaded[b.k], 16)
                if b := batch(LAG_OUT):
                    wait(sp, result_ready, b.at + 1)
                    sp.dma_start(out_dram[b.at], result[:, b.k]).then_inc(stored[b.k], 16)

            step(lambda lag: Batch(0, 0) if lag == -2 else None)
            sp.dma_start(had_raw[:, :, :], hadamard_dram).then_inc(had_loaded, 16)
            step(lambda lag: Batch(0, 1) if lag == -2 else None)
            sp.dma_start(w_raw[:, :, :], weight_dram).then_inc(weight_loaded, 16)
            for i in range(2 * LOOP_FROM):
                step(peeled(i))
            with sp.Fori(LOOP_FROM, B // 2 - 1) as half:
                for odd in range(2):
                    step(looped(half, odd))
            for i in range(B - 2, B + LAG_OUT):
                step(peeled(i))
            for k in range(2):
                sp.wait_ge(stored[k], 16 * (B // 2))

        @block.gpsimd
        def _(pool):
            nc.gpsimd.iota(stage_id[:, :], pattern=[[0, 1]], base=0, channel_multiplier=1,
                           allow_small_or_imprecise_dtypes=True).then_inc(ids_ready, 1)
            nc.gpsimd.memset(ones[:, :], 1.0).then_inc(ones_ready, 1)
            pool.wait_ge(bias_ready, 1)

            def step(batch):
                if b := batch(-1):
                    wait(pool, x_loaded[b.k], 16 * b.half + 16)
                    wait(pool, q_in_bank, b.at - 1)
                    nc.gpsimd.tensor_tensor(
                        q_nat[:, b.k], x_all[:, b.at].rearrange("p (t d) -> p t d", t=T),
                        bias[:, b.at].unsqueeze(2).broadcast_to([P, T, D]), ALU.add
                    ).then_inc(q_ready, 1)
                if b := batch(LAG_OUT):
                    wait(pool, scaled_ready, b.at + 1)
                    wait(pool, stored[b.k], 16 * b.half)
                    nc.gpsimd.tensor_tensor(
                        result[:, b.k], scaled[:, b.k].rearrange("p t d -> p (t d)"),
                        x_all[:, b.at], ALU.add).then_inc(result_ready, 1)

            for i in range(-1, 2 * LOOP_FROM):
                step(peeled(i))
            with pool.Fori(LOOP_FROM, B // 2 - 1) as half:
                for odd in range(2):
                    step(looped(half, odd))
            for i in range(B - 2, B + LAG_OUT):
                step(peeled(i))

        @block.tensor
        def _(pe):
            pe.wait_ge(one_hot_ready, 1)
            rows = embed_sb[:, :].rearrange("g (p t) -> g t p", t=T)
            for t in range(T):
                mm = pe.matmul(score_bank[:, t, 0:B], rows[:, t], one_hot[:, :], start=True, stop=True)
            mm.then_inc(bias_in_bank, 1)
            pe.wait_ge(ident_loaded, 16)

            def weights():
                pe.wait_ge(tern_ready, 1)
                for c in range(C):
                    for t in range(T):
                        mm = pe.transpose(code_bank[:, c, t * P:(t + 1) * P],
                                          tern[:, t, c * P:(c + 1) * P], ident16[:, :])
                mm.then_inc(tern_in_bank, 1)
                pe.wait_ge(diag_ready, 1)
                pe.wait_ge(ones_ready, 1)
                for t in range(T):
                    mm = pe.matmul(out_bank[:, 0, t * P:(t + 1) * P], ones[:, :], w_diag[:, t],
                                   start=True, stop=True)
                mm.then_inc(row_in_bank, 1)

            def step(batch):
                if b := batch(LAG_LOAD_TURN):
                    wait(pe, f_loaded[b.k], 16 * b.half + 16)
                    wait(pe, f_lo_ready, b.at)
                    for c in range(C):
                        for t in range(T):
                            mm = pe.transpose(f_bank[:, c, t * P:(t + 1) * P],
                                              f_nat[:, b.k, t, c * P:(c + 1) * P], ident[:, :])
                    mm.then_inc(f_in_bank, 1)
                    wait(pe, q_ready, b.at + 1)
                    wait(pe, q_lo_ready, b.at)
                    for c in range(C):
                        for t in range(T):
                            mm = pe.transpose(q_bank[:, c, t * P:(t + 1) * P],
                                              q_nat[:, b.k, t, c * P:(c + 1) * P], ident[:, :])
                    mm.then_inc(q_in_bank, 1)
                if b := batch(LAG_MIX):
                    wait(pe, prob_ready, b.at + 1)
                    wait(pe, prob_lo_ready, b.at)
                    for c in range(C):
                        for t in range(T):
                            mm = pe.transpose(prob_bank[:, c, t * P:(t + 1) * P],
                                              prob[:, t, c * P:(c + 1) * P], ident[:, :])
                    mm.then_inc(prob_in_bank, 1)
                if b := batch(LAG_SCORE):
                    wait(pe, f_lo_ready, b.at + 1)
                    wait(pe, q_lo_ready, b.at + 1)
                    wait(pe, prob_ready, b.at)
                    for t in range(T):
                        parts = [(q, g, c) for q, g in ((q_hi, f_hi), (q_hi, f_lo), (q_lo, f_hi))
                                 for c in range(C)]
                        for n, (q, g, c) in enumerate(parts):
                            mm = pe.matmul(score_bank[:, t], q[:, b.k, c, t * P:(t + 1) * P],
                                           g[:, b.k, c], start=n == 0, stop=n == len(parts) - 1)
                    mm.then_inc(score_in_bank, 1)
                if b := batch(LAG_QUANT):
                    wait(pe, code_ready, b.at + 1)
                    wait(pe, code_t_ready, b.at)
                    low = code[:, :, :].bitcast(BF16).rearrange("p t (d h) -> p t d h", h=2)
                    for c in range(C):
                        for t in range(T):
                            mm = pe.transpose(code_bank[:, c, t * P:(t + 1) * P],
                                              low[:, t, c * P:(c + 1) * P, 0], ident16[:, :])
                    mm.then_inc(code_in_bank, 1)
                if b := batch(LAG_SCORE):
                    wait(pe, fh_lo_ready, b.at)
                    for t in range(T):
                        parts = [(g, c) for g in (f_hi, f_lo) for c in range(C)]
                        for n, (g, c) in enumerate(parts):
                            mm = pe.matmul(fh_bank[:, t], g[:, b.k, c, t * P:(t + 1) * P],
                                           had[:, c], start=n == 0, stop=n == len(parts) - 1)
                    mm.then_inc(fh_in_bank, 1)
                if b := batch(LAG_MIX):
                    wait(pe, prob_lo_ready, b.at + 1)
                    wait(pe, fh_lo_ready, b.at + 1)
                    wait(pe, code_ready, b.at)
                    for t in range(T):
                        parts = [(p, g, c) for p, g in ((prob_hi, fh_hi), (prob_hi, fh_lo), (prob_lo, fh_hi))
                                 for c in range(C)]
                        for n, (p, g, c) in enumerate(parts):
                            mm = pe.matmul(xh_bank[:, t], p[:, c, t * P:(t + 1) * P],
                                           g[:, b.k, c], start=n == 0, stop=n == len(parts) - 1)
                    mm.then_inc(xh_in_bank, 1)
                if b := batch(LAG_QUANT):
                    wait(pe, code_t_ready, b.at + 1)
                    wait(pe, scaled_ready, b.at)
                    for t in range(T):
                        for c in range(C):
                            mm = pe.matmul(out_bank[:, t], code_t[:, b.k, c, t * P:(t + 1) * P],
                                           tern_t[:, c], start=c == 0, stop=c == C - 1)
                    mm.then_inc(out_in_bank, 1)

            for i in range(2 * LOOP_FROM):
                if i == LAG_SCORE:
                    pe.wait_ge(had_ready, 1)
                if i == LAG_QUANT:
                    pe.wait_ge(tern_t_ready, 1)
                    pe.wait_ge(row_ready, 1)
                step(peeled(i))
                if i == LAG_SCORE:
                    weights()
            with pe.Fori(LOOP_FROM, B // 2) as half:
                for odd in range(2):
                    step(looped(half, odd))
            for i in range(B, B + LAG_QUANT):
                step(peeled(i))

        @block.scalar
        def _(act):
            def step(batch):
                if b := batch(LAG_LOAD_TURN):
                    wait(act, fh_in_bank, b.at - 1)
                    wait(act, f_in_bank, b.at + 1)
                    nc.scalar.copy(f_hi[:, b.k], f_bank[:, :, :]).then_inc(f_hi_ready, 1)
                    wait(act, q_in_bank, b.at + 1)
                    nc.scalar.copy(q_hi[:, b.k], q_bank[:, :, :]).then_inc(q_hi_ready, 1)
                if b := batch(LAG_QUANT):
                    wait(act, inv_scale_ready, b.at + 1)
                    for t in range(T):
                        a = nc.scalar.activation(code[:, t], xh_bank[:, t], ACT.Copy, bias=MAGIC,
                                                 scale=inv_scale[:, b.k, t:t + 1])
                    a.then_inc(code_ready, 1)
                if b := batch(LAG_MIX):
                    wait(act, prob_in_bank, b.at + 1)
                    nc.scalar.copy(prob_hi[:, :, :], prob_bank[:, :, :]).then_inc(prob_hi_ready, 1)
                if b := batch(LAG_QUANT):
                    wait(act, code_in_bank, b.at + 1)
                    nc.scalar.activation(code_t[:, b.k], code_bank[:, 0:C], ACT.Copy,
                                         bias=-CODE_ONE * CODE_STEP, scale=CODE_STEP
                                         ).then_inc(code_t_ready, 1)
                if b := batch(LAG_SCORE):
                    wait(act, fh_in_bank, b.at + 1)
                    nc.scalar.copy(fh_hi[:, b.k], fh_bank[:, :, :]).then_inc(fh_hi_ready, 1)
                    wait(act, neg_max_ready, b.at + 1)
                    for t in range(T):
                        a = nc.scalar.activation(prob[:, t], score_bank[:, t], ACT.Exp,
                                                 bias=neg_max[:, b.k, t:t + 1],
                                                 accum_out=row_sum[:, b.k, t:t + 1])
                    a.then_inc(prob_ready, 1)

            for i in range(2 * LOOP_FROM):
                step(peeled(i))
            with act.Fori(LOOP_FROM, B // 2) as half:
                for odd in range(2):
                    step(looped(half, odd))
            for i in range(B, B + LAG_QUANT):
                step(peeled(i))

        @block.vector
        def _(dve):
            dve.wait_ge(bias_loaded, 32)
            dve.wait_ge(ids_ready, 1)
            nc.vector.tensor_scalar(one_hot[:, :], stage_of[:, :], stage_id[:, 0:1], None,
                                    ALU.is_equal).then_inc(one_hot_ready, 1)
            dve.wait_ge(bias_in_bank, 1)
            nc.vector.tensor_copy(bias[:, :, :].rearrange("p b t -> p t b"),
                                  score_bank[:, :, 0:B]).then_inc(bias_ready, 1)
            dve.wait_ge(ident_loaded, 16)
            nc.vector.tensor_copy(ident16[:, :], ident[:, :]).then_inc(ident16_ready, 1)

            def hadamard_part():
                dve.wait_ge(had_loaded, 16)
                nc.vector.tensor_copy(had[:, :, :], had_raw[:, :, :]).then_inc(had_ready, 1)

            def weight_parts():
                dve.wait_ge(weight_loaded, 16)
                nc.vector.tensor_reduce(w_above[:, :], w_raw[:, :, :], AX.X, ALU.add,
                                        apply_absolute_value=True).then_inc(w_step, 1)
                dve.wait_ge(w_step, 1)
                nc.vector.tensor_scalar(w_scale[:, :], w_above[:, :], 1.0 / D, MIN_ABS,
                                        ALU.mult, ALU.max).then_inc(w_step, 1)
                dve.wait_ge(w_step, 2)
                nc.vector.tensor_scalar(w_below[:, :], w_scale[:, :], -0.5, None, ALU.mult
                                        ).then_inc(w_step, 1)
                nc.vector.tensor_scalar(w_above[:, :], w_scale[:, :], 0.5, None, ALU.mult
                                        ).then_inc(w_step, 1)
                dve.wait_ge(w_step, 4)
                for t in range(T):
                    nc.vector.tensor_scalar(w_neg[:, t], w_raw[:, t], w_below[:, t:t + 1], None,
                                            ALU.is_lt).then_inc(w_step, 1)
                dve.wait_ge(w_step, 4 + T)
                for t in range(T):
                    v = nc.vector.scalar_tensor_tensor(
                        out=tern[:, t], in0=w_raw[:, t], scalar=w_above[:, t:t + 1],
                        in1=w_neg[:, t], op0=ALU.is_gt, op1=ALU.subtract)
                v.then_inc(tern_ready, 1)
                for t in range(T):
                    v = nc.vector.tensor_scalar(w_diag[:, t], ident[:, :], w_scale[:, t:t + 1], None,
                                                ALU.mult)
                v.then_inc(diag_ready, 1)

            def weight_copies():
                dve.wait_ge(tern_in_bank, 1)
                nc.vector.tensor_copy(tern_t[:, :, :], code_bank[:, 0:C]).then_inc(tern_t_ready, 1)
                dve.wait_ge(row_in_bank, 1)
                nc.vector.tensor_copy(w_scale_row[:, :], out_bank[:, 0]).then_inc(row_ready, 1)

            def split(b, low_ready, high_ready, low, source, high):
                dve.wait_ge(high_ready, b.at + 1)
                nc.vector.tensor_tensor(low, source, high.bitcast(F32), ALU.subtract
                                        ).then_inc(low_ready, 1)

            def step(batch):
                if b := batch(LAG_QUANT):
                    wait(dve, xh_in_bank, b.at + 1)
                    nc.vector.tensor_reduce(abs_max[:, :], xh_bank[:, :, :], AX.X, ALU.max,
                                            apply_absolute_value=True).then_inc(abs_max_ready, 1)
                    wait(dve, abs_max_ready, b.at + 1)
                    wait(dve, sums_ready, 2 * b.at + 2)
                    nc.vector.scalar_tensor_tensor(
                        out=raw_scale[:, :], in0=abs_max[:, :], scalar=1.0 / POS,
                        in1=least_scale[:, b.k], op0=ALU.mult, op1=ALU.max
                    ).then_inc(raw_scale_ready, 1)
                    wait(dve, raw_scale_ready, b.at + 1)
                    nc.vector.reciprocal(inv_scale[:, b.k], raw_scale[:, :]
                                         ).then_inc(inv_scale_ready, 1)
                    nc.vector.tensor_tensor(out_scale[:, b.k], raw_scale[:, :], inv_sum[:, b.k],
                                            ALU.mult).then_inc(out_scale_ready, 1)
                if b := batch(LAG_OUT):
                    wait(dve, out_in_bank, b.at + 1)
                    wait(dve, out_scale_ready, b.at + 1)
                    wait(dve, result_ready, b.at - 1)
                    for t in range(T):
                        v = nc.vector.scalar_tensor_tensor(
                            out=scaled[:, b.k, t], in0=out_bank[:, t],
                            scalar=out_scale[:, b.k, t:t + 1], in1=w_scale_row[:, :],
                            op0=ALU.mult, op1=ALU.mult)
                    v.then_inc(scaled_ready, 1)
                if b := batch(LAG_LOAD_TURN):
                    wait(dve, f_hi_ready, b.at + 1)
                    nc.vector.tensor_tensor(f_lo[:, b.k], f_bank[:, :, :], f_hi[:, b.k].bitcast(F32),
                                            ALU.subtract).then_inc(f_lo_ready, 1)
                    wait(dve, q_hi_ready, b.at + 1)
                    nc.vector.tensor_tensor(q_lo[:, b.k], q_bank[:, :, :], q_hi[:, b.k].bitcast(F32),
                                            ALU.subtract).then_inc(q_lo_ready, 1)
                if b := batch(LAG_MIX):
                    wait(dve, prob_hi_ready, b.at + 1)
                    nc.vector.tensor_tensor(prob_lo[:, :, :], prob_bank[:, :, :],
                                            prob_hi[:, :, :].bitcast(F32), ALU.subtract
                                            ).then_inc(prob_lo_ready, 1)
                    wait(dve, prob_ready, b.at + 1)
                    nc.vector.reciprocal(inv_sum[:, b.k], row_sum[:, b.k]).then_inc(sums_ready, 1)
                    nc.vector.tensor_scalar(least_scale[:, b.k], row_sum[:, b.k], MIN_ABS / POS, None,
                                            ALU.mult).then_inc(sums_ready, 1)
                if b := batch(LAG_SCORE):
                    wait(dve, score_in_bank, b.at + 1)
                    nc.vector.tensor_reduce(neg_max[:, b.k], score_bank[:, :, :], AX.X, ALU.max,
                                            negate=True).then_inc(neg_max_ready, 1)
                    wait(dve, fh_hi_ready, b.at + 1)
                    nc.vector.tensor_tensor(fh_lo[:, b.k], fh_bank[:, :, :],
                                            fh_hi[:, b.k].bitcast(F32), ALU.subtract
                                            ).then_inc(fh_lo_ready, 1)

            for i in range(2 * LOOP_FROM):
                if i == LAG_SCORE:
                    weight_copies()
                step(peeled(i))
                if i == 0:
                    hadamard_part()
                    weight_parts()
            with dve.Fori(LOOP_FROM, B // 2) as half:
                for odd in range(2):
                    step(looped(half, odd))
            for i in range(B, B + LAG_OUT):
                step(peeled(i))


def hadamard_matrix(size):
    h = np.ones((1, 1))
    while len(h) < size:
        h = np.block([[h, h], [h, -h]])
    return (h / np.sqrt(size)).astype(np.float32)


def kernel(x, fside_BxSxS_0, itok_B_0_5, L0_cond_braak_embed, L0_ffn_weight):
    import concourse.bacc as bacc
    from concourse.bass_utils import run_bass_kernel_spmd

    nc = bacc.Bacc("TRN2", target_bir_lowering=False, num_devices=1)
    arrays = {
        "x": x,
        "f": fside_BxSxS_0,
        "itok": itok_B_0_5,
        "embed": L0_cond_braak_embed,
        "weight": L0_ffn_weight,
        "identity": np.eye(P, dtype=np.float32),
        "hadamard": hadamard_matrix(x.shape[-1]),
    }
    arrays = {f"{name}_dram": np.ascontiguousarray(a) for name, a in arrays.items()}
    ins = [nc.dram_tensor(name, a.shape, mybir.dt.from_np(a.dtype), kind="ExternalInput").ap()
           for name, a in arrays.items()]
    out = nc.dram_tensor("out_dram", x.shape, F32, kind="ExternalOutput").ap()
    adaln_ffn_kernel(nc, *ins, out)
    results = run_bass_kernel_spmd(nc, [arrays], core_ids=[0]).results
    return results[0]["out_dram"]
```

```python
from contextlib import ExitStack

import numpy as np

import concourse.bass as bass
from concourse import mybir

F32 = mybir.dt.float32
F32R = mybir.dt.float32r
BF16 = mybir.dt.bfloat16
I32 = mybir.dt.int32
ALU = mybir.AluOpType
ACT = mybir.ActivationFunctionType
AX = mybir.AxisListType

P = 128

POS = 7.0
MIN_ABS = 1e-5

CODE_BITS = 0x4040
CODE_ONE = 3.0
CODE_STEP = 64.0
MAGIC = float(3 * 2**22 + CODE_BITS)

WARM = 6

LAG_LOAD_TURN = 0
LAG_SCORE = 1
LAG_MIX = 2
LAG_QUANT = 3
LAG_OUT = 4


def adaln_ffn_kernel(nc, x, f, itok, embed, weight, hadamard, out):
    B, S, D = x.shape
    STAGES = embed.shape[0]
    O = weight.shape[0]
    T = S // P
    C = D // P
    W = T * D
    assert S % P == 0 and D % P == 0 and O == D == S and W == 512 and B % 2 == 0 and B >= 8

    x_dram = x.rearrange("b (p t) d -> b p (t d)", t=T)
    f_dram = f.rearrange("b (p t) d -> b p (t d)", t=T)
    out_dram = out.rearrange("b (p t) d -> b p (t d)", t=T)
    weight_dram = weight.rearrange("(t p) d -> p t d", p=P)
    hadamard_dram = hadamard.rearrange("(c p) d -> p c d", p=P)

    with ExitStack() as ctx:
        def sb(name, shape, dtype):
            return ctx.enter_context(nc.sbuf_tensor(name, shape, dtype))

        def bank(name, shape, dtype):
            return ctx.enter_context(nc.psum_tensor(name, shape, dtype))

        def sem(name):
            return ctx.enter_context(nc.semaphore(name))

        ident = sb("ident", [P, P], F32)
        ident16 = sb("ident16", [P, P], BF16)
        warm = sb("warm", [P, W], BF16)
        ones = sb("ones", [P, P], F32)
        had_raw = sb("had_raw", [P, C, D], F32)
        had = sb("had", [P, C, D], F32R)
        w_raw = sb("w_raw", [P, T, D], F32)
        w_scale = sb("w_scale", [P, T], F32)
        w_above = sb("w_above", [P, T], F32)
        w_below = sb("w_below", [P, T], F32)
        w_neg = sb("w_neg", [P, T, D], F32)
        tern = sb("tern", [P, T, D], BF16)
        tern_t = sb("tern_t", [P, C, O], BF16)
        w_diag = sb("w_diag", [P, T, P], F32)
        w_scale_row = sb("w_scale_row", [P, O], F32)
        stage_of = sb("stage_of", [STAGES, B], I32)
        stage_id = sb("stage_id", [STAGES, 1], F32)
        one_hot = sb("one_hot", [STAGES, B], F32)
        embed_sb = sb("embed_sb", [STAGES, S], F32)
        bias = sb("bias", [P, B, T], F32)

        x_all = sb("x_all", [P, B, W], F32)
        f_nat = sb("f_nat", [P, 2, T, D], F32)
        q_nat = sb("q_nat", [P, 2, T, D], F32)
        f_hi = sb("f_hi", [P, 2, C, S], F32R)
        f_lo = sb("f_lo", [P, 2, C, S], F32R)
        q_hi = sb("q_hi", [P, 2, C, S], F32R)
        q_lo = sb("q_lo", [P, 2, C, S], F32R)
        fh_hi = sb("fh_hi", [P, 2, T, D], F32R)
        fh_lo = sb("fh_lo", [P, 2, T, D], F32R)
        neg_max = sb("neg_max", [P, 2, T], F32)
        prob = sb("prob", [P, T, S], F32)
        prob_hi = sb("prob_hi", [P, C, S], F32R)
        prob_lo = sb("prob_lo", [P, C, S], F32R)
        row_sum = sb("row_sum", [P, 2, T], F32)
        inv_sum = sb("inv_sum", [P, 2, T], F32)
        least_scale = sb("least_scale", [P, 2, T], F32)
        abs_max = sb("abs_max", [P, T], F32)
        raw_scale = sb("raw_scale", [P, T], F32)
        inv_scale = sb("inv_scale", [P, 2, T], F32)
        out_scale = sb("out_scale", [P, 2, T], F32)
        code = sb("code", [P, T, D], F32)
        code_t = sb("code_t", [P, 2, C, S], BF16)
        scaled = sb("scaled", [P, 2, T, O], F32)
        result = sb("result", [P, 2, W], F32)

        f_bank = bank("f_bank", [P, C, S], F32)
        q_bank = bank("q_bank", [P, C, S], F32)
        score_bank = bank("score_bank", [P, T, S], F32)
        fh_bank = bank("fh_bank", [P, T, D], F32)
        prob_bank = bank("prob_bank", [P, C, S], F32)
        xh_bank = bank("xh_bank", [P, T, D], F32)
        code_bank = bank("code_bank", [P, 2 * C, S], BF16)
        out_bank = bank("out_bank", [P, T, O], F32)
        tern_half = out_bank[:, T - 1].bitcast(BF16).rearrange("p (c o) -> p c o", c=C)

        ident_clear = sem("ident_clear")
        ident_ready = sem("ident_ready")
        warm_ready = sem("warm_ready")
        had_loaded = sem("had_loaded")
        weight_loaded = sem("weight_loaded")
        bias_loaded = sem("bias_loaded")
        x_loaded = [sem(f"x_loaded{k}") for k in range(2)]
        f_loaded = [sem(f"f_loaded{k}") for k in range(2)]
        stored = [sem(f"stored{k}") for k in range(2)]
        ids_ready = sem("ids_ready")
        one_hot_ready = sem("one_hot_ready")
        bias_in_bank = sem("bias_in_bank")
        bias_ready = sem("bias_ready")
        ones_ready = sem("ones_ready")
        had_ready = sem("had_ready")
        w_step = sem("w_step")
        tern_ready = sem("tern_ready")
        tern_t_ready = sem("tern_t_ready")
        diag_ready = sem("diag_ready")
        weights_in_bank = sem("weights_in_bank")
        row_ready = sem("row_ready")

        q_ready = sem("q_ready")
        f_in_bank = sem("f_in_bank")
        q_in_bank = sem("q_in_bank")
        f_hi_ready = sem("f_hi_ready")
        f_lo_ready = sem("f_lo_ready")
        q_hi_ready = sem("q_hi_ready")
        q_lo_ready = sem("q_lo_ready")
        score_in_bank = sem("score_in_bank")
        neg_max_ready = sem("neg_max_ready")
        prob_ready = sem("prob_ready")
        sums_ready = sem("sums_ready")
        fh_in_bank = sem("fh_in_bank")
        fh_hi_ready = sem("fh_hi_ready")
        fh_lo_ready = sem("fh_lo_ready")
        prob_in_bank = sem("prob_in_bank")
        prob_hi_ready = sem("prob_hi_ready")
        prob_lo_ready = sem("prob_lo_ready")
        xh_in_bank = sem("xh_in_bank")
        abs_max_ready = sem("abs_max_ready")
        raw_scale_ready = sem("raw_scale_ready")
        inv_scale_ready = sem("inv_scale_ready")
        out_scale_ready = sem("out_scale_ready")
        code_ready = sem("code_ready")
        code_in_bank = sem("code_in_bank")
        code_t_ready = sem("code_t_ready")
        out_in_bank = sem("out_in_bank")
        scaled_ready = sem("scaled_ready")
        result_ready = sem("result_ready")

        block = ctx.enter_context(nc.Block())

        class Batch:

            def __init__(self, half, odd):
                self.half, self.k = half + odd // 2, odd % 2
                self.at = 2 * self.half + self.k

        LOOP_FROM = LAG_OUT // 2 + 1

        def peeled(i):
            return lambda lag: Batch(0, i - lag) if 0 <= i - lag < B else None

        def looped(half, odd):
            return lambda lag: Batch(half, odd - lag)

        def wait(engine, semaphore, count):
            if not (isinstance(count, int) and count <= 0):
                engine.wait_ge(semaphore, count)

        @block.sync
        def _(sp):
            sp.dma_start(f_nat[:, 0], f_dram[0]).then_inc(f_loaded[0], 16)
            sp.dma_start(embed_sb[:, :], embed).then_inc(bias_loaded, 16)
            sp.dma_start(x_all[:, 0], x_dram[0]).then_inc(x_loaded[0], 16)
            sp.dma_start(had_raw[:, :, :], hadamard_dram).then_inc(had_loaded, 16)
            sp.dma_start(f_nat[:, 1], f_dram[1]).then_inc(f_loaded[1], 16)
            sp.dma_start(x_all[:, 1], x_dram[1]).then_inc(x_loaded[1], 16)
            sp.dma_start(w_raw[:, :, :], weight_dram).then_inc(weight_loaded, 16)

            def step(batch):
                if b := batch(-2):
                    wait(sp, f_in_bank, b.at - 1)
                    sp.dma_start(f_nat[:, b.k], f_dram[b.at]).then_inc(f_loaded[b.k], 16)
                    wait(sp, q_ready, b.at - 1)
                    sp.dma_start(x_all[:, b.at], x_dram[b.at]).then_inc(x_loaded[b.k], 16)
                if b := batch(LAG_OUT):
                    wait(sp, result_ready, b.at + 1)
                    sp.dma_start(out_dram[b.at], result[:, b.k]).then_inc(stored[b.k], 16)

            for i in range(2 * LOOP_FROM):
                step(peeled(i))
            with sp.Fori(LOOP_FROM, B // 2 - 1) as half:
                for odd in range(2):
                    step(looped(half, odd))
            for i in range(B - 2, B + LAG_OUT):
                step(peeled(i))
            for k in range(2):
                sp.wait_ge(stored[k], 16 * (B // 2))

        @block.gpsimd
        def _(pool):
            nc.gpsimd.iota(stage_id[:, :], pattern=[[0, 1]], base=0, channel_multiplier=1,
                           allow_small_or_imprecise_dtypes=True).then_inc(ids_ready, 1)
            nc.gpsimd.memset(ident[:, :], 0.0).then_inc(ident_clear, 1)
            nc.gpsimd.memset(ident16[:, :], 0.0).then_inc(ident_clear, 1)
            pool.wait_ge(ident_clear, 2)
            for square in (ident, ident16):
                nc.gpsimd.affine_select(out=square[:, :], in_=square[:, :], compare_op=ALU.not_equal,
                                        fill=1.0, base=0, pattern=[[1, P]], channel_multiplier=-1
                                        ).then_inc(ident_ready, 1)
            nc.gpsimd.memset(ones[:, :], 1.0).then_inc(ones_ready, 1)
            pool.wait_ge(bias_ready, 1)
            pool.wait_ge(q_ready, 1)

            def step(batch):
                if b := batch(-1):
                    wait(pool, x_loaded[b.k], 16 * b.half + 16)
                    wait(pool, q_in_bank, b.at - 1)
                    nc.gpsimd.tensor_tensor(
                        q_nat[:, b.k], x_all[:, b.at].rearrange("p (t d) -> p t d", t=T),
                        bias[:, b.at].unsqueeze(2).broadcast_to([P, T, D]), ALU.add
                    ).then_inc(q_ready, 1)
                if b := batch(LAG_OUT):
                    wait(pool, scaled_ready, b.at + 1)
                    wait(pool, stored[b.k], 16 * b.half)
                    nc.gpsimd.tensor_tensor(
                        result[:, b.k], scaled[:, b.k].rearrange("p t d -> p (t d)"),
                        x_all[:, b.at], ALU.add).then_inc(result_ready, 1)

            for i in range(2 * LOOP_FROM):
                step(peeled(i))
            with pool.Fori(LOOP_FROM, B // 2 - 1) as half:
                for odd in range(2):
                    step(looped(half, odd))
            for i in range(B - 2, B + LAG_OUT):
                step(peeled(i))

        @block.tensor
        def _(pe):
            pe.wait_ge(warm_ready, 1)

            def keep_warm(products):
                for _ in range(products):
                    pe.matmul(out_bank[:, :, :], warm[:, 0:P], warm[:, :], start=True, stop=True)

            keep_warm(WARM)
            pe.wait_ge(ident_ready, 2)

            def bias_product():
                pe.wait_ge(one_hot_ready, 1)
                rows = embed_sb[:, :].rearrange("g (p t) -> g t p", t=T)
                for t in range(T):
                    mm = pe.matmul(score_bank[:, t, 0:B], rows[:, t], one_hot[:, :],
                                   start=True, stop=True)
                mm.then_inc(bias_in_bank, 1)

            def weights():
                pe.wait_ge(tern_ready, 1)
                for c in range(C):
                    for t in range(T):
                        pe.transpose(tern_half[:, c, t * P:(t + 1) * P],
                                     tern[:, t, c * P:(c + 1) * P], ident16[:, :])
                pe.wait_ge(diag_ready, 1)
                pe.wait_ge(ones_ready, 1)
                for t in range(T):
                    mm = pe.matmul(out_bank[:, 0, t * P:(t + 1) * P], ones[:, :], w_diag[:, t],
                                   start=True, stop=True)
                mm.then_inc(weights_in_bank, 1)

            def turn(to, of, by):
                for c in range(C):
                    for t in range(T):
                        mm = pe.transpose(to[:, c, t * P:(t + 1) * P], of[:, t, c * P:(c + 1) * P], by)
                return mm

            def product(to, parts):
                for t in range(T):
                    terms = [(left, right, c) for left, right in parts for c in range(C)]
                    for n, (left, right, c) in enumerate(terms):
                        mm = pe.matmul(to[:, t], left[:, c, t * P:(t + 1) * P], right[:, c],
                                       start=n == 0, stop=n == len(terms) - 1)
                return mm

            def turn_f(b):
                wait(pe, f_loaded[b.k], 16 * b.half + 16)
                wait(pe, f_lo_ready, b.at)
                turn(f_bank, f_nat[:, b.k], ident[:, :]).then_inc(f_in_bank, 1)

            def turn_q(b):
                wait(pe, q_ready, b.at + 1)
                wait(pe, q_lo_ready, b.at)
                turn(q_bank, q_nat[:, b.k], ident[:, :]).then_inc(q_in_bank, 1)

            def turn_prob(b):
                wait(pe, prob_ready, b.at + 1)
                wait(pe, prob_lo_ready, b.at)
                turn(prob_bank, prob, ident[:, :]).then_inc(prob_in_bank, 1)

            def score(b):
                wait(pe, f_lo_ready, b.at + 1)
                wait(pe, q_lo_ready, b.at + 1)
                wait(pe, prob_ready, b.at)
                product(score_bank, [(q_hi[:, b.k], f_hi[:, b.k]), (q_hi[:, b.k], f_lo[:, b.k]),
                                     (q_lo[:, b.k], f_hi[:, b.k])]).then_inc(score_in_bank, 1)

            def turn_code(b):
                wait(pe, code_ready, b.at + 1)
                wait(pe, code_t_ready, b.at)
                low = code[:, :, :].bitcast(BF16).rearrange("p t (d h) -> p t d h", h=2)
                turn(code_bank, low[:, :, :, 0], ident16[:, :]).then_inc(code_in_bank, 1)

            def times_hadamard(b):
                wait(pe, f_lo_ready, b.at + 1)
                wait(pe, fh_lo_ready, b.at)
                product(fh_bank, [(f_hi[:, b.k], had), (f_lo[:, b.k], had)]).then_inc(fh_in_bank, 1)

            def mix(b):
                wait(pe, prob_lo_ready, b.at + 1)
                wait(pe, fh_lo_ready, b.at + 1)
                wait(pe, code_ready, b.at)
                product(xh_bank, [(prob_hi, fh_hi[:, b.k]), (prob_hi, fh_lo[:, b.k]),
                                  (prob_lo, fh_hi[:, b.k])]).then_inc(xh_in_bank, 1)

            def times_ternary(b):
                wait(pe, code_t_ready, b.at + 1)
                wait(pe, scaled_ready, b.at)
                product(out_bank, [(code_t[:, b.k], tern_t)]).then_inc(out_in_bank, 1)

            STAGES_IN_ORDER = (
                (turn_f, LAG_LOAD_TURN), (turn_q, LAG_LOAD_TURN), (turn_prob, LAG_MIX),
                (score, LAG_SCORE), (turn_code, LAG_QUANT), (times_hadamard, LAG_SCORE),
                (mix, LAG_MIX), (times_ternary, LAG_QUANT))

            def step(batch):
                for stage, lag in STAGES_IN_ORDER:
                    if b := batch(lag):
                        stage(b)

            b0, b1, b2 = (Batch(0, n) for n in range(3))
            turn_f(b0)
            bias_product()
            keep_warm(3)
            turn_q(b0)
            pe.wait_ge(had_ready, 1)
            times_hadamard(b0)
            turn_f(b1)
            pe.wait_ge(bias_ready, 1)
            score(b0)
            turn_q(b1)
            turn_f(b2)
            times_hadamard(b1)
            turn_prob(b0)
            turn_q(b2)
            score(b1)
            mix(b0)
            for stage, lag in STAGES_IN_ORDER:
                if b := peeled(3)(lag):
                    if stage == times_hadamard:
                        weights()
                    if stage == times_ternary:
                        pe.wait_ge(tern_t_ready, 1)
                        pe.wait_ge(row_ready, 1)
                    stage(b)
            for i in range(4, 2 * LOOP_FROM):
                step(peeled(i))
            with pe.Fori(LOOP_FROM, B // 2) as half:
                for odd in range(2):
                    step(looped(half, odd))
            b13, b14, b15 = (Batch(0, B - n) for n in (3, 2, 1))
            turn_prob(b14)
            score(b15)
            turn_code(b13)
            times_hadamard(b15)
            mix(b14)
            turn_prob(b15)
            times_ternary(b13)
            mix(b15)
            turn_code(b14)
            times_ternary(b14)
            turn_code(b15)
            times_ternary(b15)

        @block.scalar
        def _(act):
            act.dma_start(stage_of[:, :], itok.partition_broadcast(STAGES)).then_inc(bias_loaded, 16)
            act.wait_ge(warm_ready, 1)
            nc.scalar.activation(row_sum[:, 0], warm[:, 0:T], ACT.Exp)

            def split_f(b):
                wait(act, fh_in_bank, b.at - 1)
                wait(act, f_in_bank, b.at + 1)
                nc.scalar.copy(f_hi[:, b.k], f_bank[:, :, :]).then_inc(f_hi_ready, 1)

            def split_q(b):
                wait(act, q_in_bank, b.at + 1)
                nc.scalar.copy(q_hi[:, b.k], q_bank[:, :, :]).then_inc(q_hi_ready, 1)

            def quantize(b):
                wait(act, inv_scale_ready, b.at + 1)
                for t in range(T):
                    a = nc.scalar.activation(code[:, t], xh_bank[:, t], ACT.Copy, bias=MAGIC,
                                             scale=inv_scale[:, b.k, t:t + 1])
                a.then_inc(code_ready, 1)

            def split_prob(b):
                wait(act, prob_in_bank, b.at + 1)
                nc.scalar.copy(prob_hi[:, :, :], prob_bank[:, :, :]).then_inc(prob_hi_ready, 1)

            def decode(b):
                wait(act, code_in_bank, b.at + 1)
                nc.scalar.activation(code_t[:, b.k], code_bank[:, 0:C], ACT.Copy,
                                     bias=-CODE_ONE * CODE_STEP, scale=CODE_STEP
                                     ).then_inc(code_t_ready, 1)

            def split_fh(b):
                wait(act, fh_in_bank, b.at + 1)
                nc.scalar.copy(fh_hi[:, b.k], fh_bank[:, :, :]).then_inc(fh_hi_ready, 1)

            def exponentials(b):
                wait(act, neg_max_ready, b.at + 1)
                for t in range(T):
                    a = nc.scalar.activation(prob[:, t], score_bank[:, t], ACT.Exp,
                                             bias=neg_max[:, b.k, t:t + 1],
                                             accum_out=row_sum[:, b.k, t:t + 1])
                a.then_inc(prob_ready, 1)

            STAGES_IN_ORDER = (
                (split_f, LAG_LOAD_TURN), (split_q, LAG_LOAD_TURN), (quantize, LAG_QUANT),
                (split_prob, LAG_MIX), (decode, LAG_QUANT), (split_fh, LAG_SCORE),
                (exponentials, LAG_SCORE))

            def step(batch):
                for stage, lag in STAGES_IN_ORDER:
                    if b := batch(lag):
                        stage(b)

            b0, b1, b2 = (Batch(0, n) for n in range(3))
            split_f(b0)
            act.wait_ge(had_loaded, 16)
            nc.scalar.copy(had[:, :, :], had_raw[:, :, :]).then_inc(had_ready, 1)
            split_q(b0)
            split_fh(b0)
            split_f(b1)
            split_q(b1)
            exponentials(b0)
            split_f(b2)
            split_fh(b1)
            split_prob(b0)
            split_q(b2)
            act.wait_ge(w_step, 2)
            for t in range(T):
                a = nc.scalar.activation(w_diag[:, t], ident[:, :], ACT.Copy, scale=w_scale[:, t:t + 1])
            a.then_inc(diag_ready, 1)
            exponentials(b1)
            for i in range(3, 2 * LOOP_FROM):
                step(peeled(i))
            with act.Fori(LOOP_FROM, B // 2) as half:
                for odd in range(2):
                    step(looped(half, odd))
            b13, b14, b15 = (Batch(0, B - n) for n in (3, 2, 1))
            quantize(b13)
            split_prob(b14)
            decode(b13)
            exponentials(b15)
            split_fh(b15)
            split_prob(b15)
            quantize(b14)
            decode(b14)
            quantize(b15)
            decode(b15)

        @block.vector
        def _(dve):
            nc.vector.memset(warm[:, :], 0.0).then_inc(warm_ready, 1)
            dve.wait_ge(bias_loaded, 32)
            dve.wait_ge(ids_ready, 1)
            nc.vector.tensor_scalar(one_hot[:, :], stage_of[:, :], stage_id[:, 0:1], None,
                                    ALU.is_equal).then_inc(one_hot_ready, 1)
            dve.wait_ge(bias_in_bank, 1)
            nc.vector.tensor_copy(bias[:, :, :].rearrange("p b t -> p t b"),
                                  score_bank[:, :, 0:B]).then_inc(bias_ready, 1)

            def weight_scales():
                dve.wait_ge(weight_loaded, 16)
                nc.vector.tensor_reduce(w_above[:, :], w_raw[:, :, :], AX.X, ALU.add,
                                        apply_absolute_value=True).then_inc(w_step, 1)
                dve.wait_ge(w_step, 1)
                nc.vector.tensor_scalar(w_scale[:, :], w_above[:, :], 1.0 / D, MIN_ABS,
                                        ALU.mult, ALU.max).then_inc(w_step, 1)
                dve.wait_ge(w_step, 2)
                nc.vector.tensor_scalar(w_below[:, :], w_scale[:, :], -0.5, None, ALU.mult
                                        ).then_inc(w_step, 1)
                nc.vector.tensor_scalar(w_above[:, :], w_scale[:, :], 0.5, None, ALU.mult
                                        ).then_inc(w_step, 1)

            def weight_signs():
                dve.wait_ge(w_step, 4)
                for t in range(T):
                    nc.vector.tensor_scalar(w_neg[:, t], w_raw[:, t], w_below[:, t:t + 1], None,
                                            ALU.is_lt).then_inc(w_step, 1)
                dve.wait_ge(w_step, 4 + T)
                for t in range(T):
                    v = nc.vector.scalar_tensor_tensor(
                        out=tern[:, t], in0=w_raw[:, t], scalar=w_above[:, t:t + 1],
                        in1=w_neg[:, t], op0=ALU.is_gt, op1=ALU.subtract)
                v.then_inc(tern_ready, 1)

            def weight_copies():
                dve.wait_ge(weights_in_bank, 1)
                nc.vector.tensor_copy(tern_t[:, :, :], tern_half).then_inc(tern_t_ready, 1)
                nc.vector.tensor_copy(w_scale_row[:, :], out_bank[:, 0]).then_inc(row_ready, 1)

            def scales(b):
                wait(dve, xh_in_bank, b.at + 1)
                nc.vector.tensor_reduce(abs_max[:, :], xh_bank[:, :, :], AX.X, ALU.max,
                                        apply_absolute_value=True).then_inc(abs_max_ready, 1)
                wait(dve, abs_max_ready, b.at + 1)
                wait(dve, sums_ready, 2 * b.at + 2)
                nc.vector.scalar_tensor_tensor(
                    out=raw_scale[:, :], in0=abs_max[:, :], scalar=1.0 / POS,
                    in1=least_scale[:, b.k], op0=ALU.mult, op1=ALU.max
                ).then_inc(raw_scale_ready, 1)
                wait(dve, raw_scale_ready, b.at + 1)
                nc.vector.reciprocal(inv_scale[:, b.k], raw_scale[:, :]).then_inc(inv_scale_ready, 1)
                nc.vector.tensor_tensor(out_scale[:, b.k], raw_scale[:, :], inv_sum[:, b.k],
                                        ALU.mult).then_inc(out_scale_ready, 1)

            def scale_out(b):
                wait(dve, out_in_bank, b.at + 1)
                wait(dve, out_scale_ready, b.at + 1)
                wait(dve, result_ready, b.at - 1)
                for t in range(T):
                    v = nc.vector.scalar_tensor_tensor(
                        out=scaled[:, b.k, t], in0=out_bank[:, t],
                        scalar=out_scale[:, b.k, t:t + 1], in1=w_scale_row[:, :],
                        op0=ALU.mult, op1=ALU.mult)
                v.then_inc(scaled_ready, 1)

            def low_part(low, of, high):
                return nc.vector.tensor_tensor(low, of[:, :, :], high.bitcast(F32), ALU.subtract)

            def split_f(b):
                wait(dve, f_hi_ready, b.at + 1)
                low_part(f_lo[:, b.k], f_bank, f_hi[:, b.k]).then_inc(f_lo_ready, 1)

            def split_q(b):
                wait(dve, q_hi_ready, b.at + 1)
                low_part(q_lo[:, b.k], q_bank, q_hi[:, b.k]).then_inc(q_lo_ready, 1)

            def split_prob(b):
                wait(dve, prob_hi_ready, b.at + 1)
                low_part(prob_lo[:, :, :], prob_bank, prob_hi[:, :, :]).then_inc(prob_lo_ready, 1)

            def split_fh(b):
                wait(dve, fh_hi_ready, b.at + 1)
                low_part(fh_lo[:, b.k], fh_bank, fh_hi[:, b.k]).then_inc(fh_lo_ready, 1)

            def sums(b):
                wait(dve, prob_ready, b.at + 1)
                nc.vector.reciprocal(inv_sum[:, b.k], row_sum[:, b.k]).then_inc(sums_ready, 1)
                nc.vector.tensor_scalar(least_scale[:, b.k], row_sum[:, b.k], MIN_ABS / POS, None,
                                        ALU.mult).then_inc(sums_ready, 1)

            def maximum(b):
                wait(dve, score_in_bank, b.at + 1)
                nc.vector.tensor_reduce(neg_max[:, b.k], score_bank[:, :, :], AX.X, ALU.max,
                                        negate=True).then_inc(neg_max_ready, 1)

            STAGES_IN_ORDER = (
                (scales, LAG_QUANT), (scale_out, LAG_OUT), (split_f, LAG_LOAD_TURN),
                (split_q, LAG_LOAD_TURN), (split_prob, LAG_MIX), (sums, LAG_MIX),
                (maximum, LAG_SCORE), (split_fh, LAG_SCORE))

            def step(batch):
                for stage, lag in STAGES_IN_ORDER:
                    if b := batch(lag):
                        stage(b)

            dve.wait_ge(x_loaded[0], 16)
            dve.wait_ge(bias_ready, 1)
            nc.vector.tensor_tensor(
                q_nat[:, 0], x_all[:, 0].rearrange("p (t d) -> p t d", t=T),
                bias[:, 0].unsqueeze(2).broadcast_to([P, T, D]), ALU.add).then_inc(q_ready, 1)
            b0, b1, b2 = (Batch(0, n) for n in range(3))
            split_f(b0)
            split_q(b0)
            split_fh(b0)
            split_f(b1)
            maximum(b0)
            split_q(b1)
            weight_scales()
            split_f(b2)
            split_fh(b1)
            split_prob(b0)
            sums(b0)
            split_q(b2)
            maximum(b1)
            weight_signs()
            for stage, lag in STAGES_IN_ORDER:
                if b := peeled(3)(lag):
                    if stage == split_fh:
                        weight_copies()
                    stage(b)
            for i in range(4, 2 * LOOP_FROM):
                step(peeled(i))
            with dve.Fori(LOOP_FROM, B // 2) as half:
                for odd in range(2):
                    step(looped(half, odd))
            b12, b13, b14, b15 = (Batch(0, B - n) for n in (4, 3, 2, 1))
            scales(b13)
            scale_out(b12)
            maximum(b15)
            split_prob(b14)
            sums(b14)
            split_fh(b15)
            scales(b14)
            split_prob(b15)
            sums(b15)
            scale_out(b13)
            scales(b15)
            scale_out(b14)
            scale_out(b15)


def hadamard_matrix(size):
    h = np.ones((1, 1))
    while len(h) < size:
        h = np.block([[h, h], [h, -h]])
    return (h / np.sqrt(size)).astype(np.float32)


def kernel(x, fside_BxSxS_0, itok_B_0_5, L0_cond_braak_embed, L0_ffn_weight):
    import concourse.bacc as bacc
    from concourse.bass_utils import run_bass_kernel_spmd

    nc = bacc.Bacc("TRN2", target_bir_lowering=False, num_devices=1)
    arrays = {
        "x": x,
        "f": fside_BxSxS_0,
        "itok": itok_B_0_5,
        "embed": L0_cond_braak_embed,
        "weight": L0_ffn_weight,
        "hadamard": hadamard_matrix(x.shape[-1]),
    }
    arrays = {f"{name}_dram": np.ascontiguousarray(a) for name, a in arrays.items()}
    ins = [nc.dram_tensor(name, a.shape, mybir.dt.from_np(a.dtype), kind="ExternalInput").ap()
           for name, a in arrays.items()]
    out = nc.dram_tensor("out_dram", x.shape, F32, kind="ExternalOutput").ap()
    adaln_ffn_kernel(nc, *ins, out)
    results = run_bass_kernel_spmd(nc, [arrays], core_ids=[0]).results
    return results[0]["out_dram"]
```

```python
from contextlib import ExitStack

import numpy as np

import concourse.bass as bass
from concourse import mybir

F32 = mybir.dt.float32
F32R = mybir.dt.float32r
BF16 = mybir.dt.bfloat16
I32 = mybir.dt.int32
ALU = mybir.AluOpType
ACT = mybir.ActivationFunctionType
AX = mybir.AxisListType

P = 128

POS = 7.0
MIN_ABS = 1e-5

CODE_BITS = 0x4040
CODE_ONE = 3.0
CODE_STEP = 64.0
MAGIC = float(3 * 2**22 + CODE_BITS)

WARM = 7

LAG_LOAD_TURN = 0
LAG_SCORE = 1
LAG_MIX = 2
LAG_QUANT = 3
LAG_OUT = 4


def adaln_ffn_kernel(nc, x, f, itok, embed, weight, hadamard, out):
    B, S, D = x.shape
    STAGES = embed.shape[0]
    O = weight.shape[0]
    T = S // P
    C = D // P
    W = T * D
    assert S % P == 0 and D % P == 0 and O == D == S and W == 512 and B % 2 == 0 and B >= 8

    x_dram = x.rearrange("b (p t) d -> b p (t d)", t=T)
    f_dram = f.rearrange("b (p t) d -> b p (t d)", t=T)
    out_dram = out.rearrange("b (p t) d -> b p (t d)", t=T)
    weight_dram = weight.rearrange("(t p) d -> p t d", p=P)
    hadamard_dram = hadamard.rearrange("(c p) d -> p c d", p=P)

    with ExitStack() as ctx:
        def sb(name, shape, dtype):
            return ctx.enter_context(nc.sbuf_tensor(name, shape, dtype))

        def bank(name, shape, dtype):
            return ctx.enter_context(nc.psum_tensor(name, shape, dtype))

        def sem(name):
            return ctx.enter_context(nc.semaphore(name))

        ident = sb("ident", [P, P], F32)
        ident16 = sb("ident16", [P, P], BF16)
        warm = sb("warm", [P, W], BF16)
        ones = sb("ones", [P, P], F32)
        had_raw = sb("had_raw", [P, C, D], F32)
        had = sb("had", [P, C, D], F32R)
        w_raw = sb("w_raw", [P, T, D], F32)
        w_scale = sb("w_scale", [P, T], F32)
        w_above = sb("w_above", [P, T], F32)
        w_below = sb("w_below", [P, T], F32)
        w_abs = sb("w_abs", [P, T, D], F32)
        w_sum = sb("w_sum", [P, T], F32)
        w_neg = sb("w_neg", [P, T, D], F32)
        w_pos = sb("w_pos", [P, T, D], F32)
        tern = sb("tern", [P, T, D], BF16)
        tern_t = sb("tern_t", [P, C, O], BF16)
        w_diag = sb("w_diag", [P, T, P], F32)
        w_scale_row = sb("w_scale_row", [P, O], F32)
        stage_of = sb("stage_of", [STAGES, B], I32)
        stage_id = sb("stage_id", [STAGES, 1], F32)
        one_hot = sb("one_hot", [STAGES, B], F32)
        embed_sb = sb("embed_sb", [STAGES, S], F32)
        bias = sb("bias", [P, B, T], F32)

        x_all = sb("x_all", [P, B, W], F32)
        f_nat = sb("f_nat", [P, 2, T, D], F32)
        q_nat = sb("q_nat", [P, 2, T, D], F32)
        f_hi = sb("f_hi", [P, 2, C, S], F32R)
        f_lo = sb("f_lo", [P, 2, C, S], F32R)
        q_hi = sb("q_hi", [P, 2, C, S], F32R)
        q_lo = sb("q_lo", [P, 2, C, S], F32R)
        fh_hi = sb("fh_hi", [P, 2, T, D], F32R)
        fh_lo = sb("fh_lo", [P, 2, T, D], F32R)
        neg_max = sb("neg_max", [P, 2, T], F32)
        prob = sb("prob", [P, T, S], F32)
        prob_hi = sb("prob_hi", [P, 2, C, S], F32R)
        prob_lo = sb("prob_lo", [P, 2, C, S], F32R)
        row_sum = sb("row_sum", [P, 2, T], F32)
        inv_sum = sb("inv_sum", [P, 2, T], F32)
        least_scale = sb("least_scale", [P, 2, T], F32)
        abs_max = sb("abs_max", [P, T], F32)
        raw_scale = sb("raw_scale", [P, T], F32)
        inv_scale = sb("inv_scale", [P, 2, T], F32)
        out_scale = sb("out_scale", [P, 2, T], F32)
        last_out_scale = sb("last_out_scale", [P, T], F32)
        code = sb("code", [P, T, D], F32)
        last_code = sb("last_code", [P, T, D], F32)
        code_t = sb("code_t", [P, 2, C, S], BF16)
        scaled = sb("scaled", [P, 2, T, O], F32)
        result = sb("result", [P, 2, W], F32)

        f_bank = bank("f_bank", [P, C, S], F32)
        q_bank = bank("q_bank", [P, C, S], F32)
        score_bank = bank("score_bank", [P, T, S], F32)
        fh_bank = bank("fh_bank", [P, T, D], F32)
        prob_bank = bank("prob_bank", [P, C, S], F32)
        xh_bank = bank("xh_bank", [P, T, D], F32)
        code_bank = bank("code_bank", [P, 2 * C, S], BF16)
        out_bank = bank("out_bank", [P, T, O], F32)
        tern_half = out_bank[:, T - 1].bitcast(BF16).rearrange("p (c o) -> p c o", c=C)

        last_xh_banks = [f_bank, q_bank]
        last_code_banks = [xh_bank[:, :, :].bitcast(BF16), score_bank[:, :, :].bitcast(BF16)]
        last_out_banks = [fh_bank, prob_bank]
        second_last_out_banks = [f_bank, out_bank]

        ident_clear = sem("ident_clear")
        ident_ready = sem("ident_ready")
        warm_ready = sem("warm_ready")
        had_loaded = sem("had_loaded")
        weight_loaded = sem("weight_loaded")
        bias_loaded = sem("bias_loaded")
        x_loaded = [sem(f"x_loaded{k}") for k in range(2)]
        f_loaded = [sem(f"f_loaded{k}") for k in range(2)]
        stored = [sem(f"stored{k}") for k in range(2)]
        ids_ready = sem("ids_ready")
        one_hot_ready = sem("one_hot_ready")
        bias_in_bank = sem("bias_in_bank")
        bias_ready = sem("bias_ready")
        ones_ready = sem("ones_ready")
        had_ready = sem("had_ready")
        w_sums_ready = sem("w_sums_ready")
        w_scale_ready = sem("w_scale_ready")
        w_bounds_ready = sem("w_bounds_ready")
        w_signs_ready = sem("w_signs_ready")
        tern_ready = sem("tern_ready")
        tern_t_ready = sem("tern_t_ready")
        diag_ready = sem("diag_ready")
        weights_in_bank = sem("weights_in_bank")
        row_ready = sem("row_ready")

        q_ready = sem("q_ready")
        f_in_bank = sem("f_in_bank")
        q_in_bank = sem("q_in_bank")
        f_hi_ready = sem("f_hi_ready")
        f_lo_ready = sem("f_lo_ready")
        q_hi_ready = sem("q_hi_ready")
        q_lo_ready = sem("q_lo_ready")
        score_in_bank = sem("score_in_bank")
        neg_max_ready = sem("neg_max_ready")
        prob_ready = sem("prob_ready")
        sums_ready = sem("sums_ready")
        fh_in_bank = sem("fh_in_bank")
        fh_hi_ready = sem("fh_hi_ready")
        fh_lo_ready = sem("fh_lo_ready")
        prob_in_bank = sem("prob_in_bank")
        prob_hi_ready = sem("prob_hi_ready")
        prob_lo_ready = sem("prob_lo_ready")
        xh_in_bank = sem("xh_in_bank")
        abs_max_ready = sem("abs_max_ready")
        raw_scale_ready = sem("raw_scale_ready")
        inv_scale_ready = sem("inv_scale_ready")
        out_scale_ready = sem("out_scale_ready")
        code_ready = sem("code_ready")
        code_in_bank = sem("code_in_bank")
        code_t_ready = sem("code_t_ready")
        out_in_bank = sem("out_in_bank")
        scaled_ready = sem("scaled_ready")
        result_ready = sem("result_ready")
        last_xh_in_bank = sem("last_xh_in_bank")
        last_abs_ready = sem("last_abs_ready")
        last_code_ready = sem("last_code_ready")
        last_code_in_bank = sem("last_code_in_bank")
        last_code_t_ready = sem("last_code_t_ready")
        tiles_out_in_bank = sem("tiles_out_in_bank")
        tiles_scaled = sem("tiles_scaled")
        tile_results_ready = sem("tile_results_ready")
        columns_scaled = sem("columns_scaled")
        last_result_ready = sem("last_result_ready")

        def as_rows(tiles):
            return tiles.rearrange("p t d -> p (t d)")

        block = ctx.enter_context(nc.Block())

        class Batch:

            def __init__(self, half, odd):
                self.half, self.k = half + odd // 2, odd % 2
                self.at = 2 * self.half + self.k

        LOOP_FROM = LAG_OUT // 2 + 1

        def peeled(i):
            return lambda lag: Batch(0, i - lag) if 0 <= i - lag < B else None

        def looped(half, odd):
            return lambda lag: Batch(half, odd - lag)

        def wait(engine, semaphore, count):
            if not (isinstance(count, int) and count <= 0):
                engine.wait_ge(semaphore, count)

        @block.sync
        def _(sp):
            sp.dma_start(f_nat[:, 0], f_dram[0]).then_inc(f_loaded[0], 16)
            sp.dma_start(embed_sb[:, :], embed).then_inc(bias_loaded, 16)
            sp.dma_start(x_all[:, 0], x_dram[0]).then_inc(x_loaded[0], 16)
            sp.dma_start(had_raw[:, :, :], hadamard_dram).then_inc(had_loaded, 16)
            sp.dma_start(f_nat[:, 1], f_dram[1]).then_inc(f_loaded[1], 16)
            sp.dma_start(x_all[:, 1], x_dram[1]).then_inc(x_loaded[1], 16)
            sp.dma_start(w_raw[:, :, :], weight_dram).then_inc(weight_loaded, 16)

            def step(batch):
                if b := batch(-2):
                    wait(sp, f_in_bank, b.at - 1)
                    sp.dma_start(f_nat[:, b.k], f_dram[b.at]).then_inc(f_loaded[b.k], 16)
                    wait(sp, q_ready, b.at - 1)
                    sp.dma_start(x_all[:, b.at], x_dram[b.at]).then_inc(x_loaded[b.k], 16)
                if b := batch(LAG_OUT):
                    wait(sp, result_ready, b.at + 1)
                    sp.dma_start(out_dram[b.at], result[:, b.k]).then_inc(stored[b.k], 16)

            for i in range(2 * LOOP_FROM):
                step(peeled(i))
            with sp.Fori(LOOP_FROM, B // 2 - 1) as half:
                for odd in range(2):
                    step(looped(half, odd))
            for i in range(B - 2, B + LAG_OUT - 2):
                step(peeled(i))
            second_last, last = Batch(0, B - 2), Batch(0, B - 1)
            for t in range(T):
                sp.wait_ge(tile_results_ready, t + 1)
                cols = slice(t * D, (t + 1) * D)
                sp.dma_start(out_dram[second_last.at, :, cols], result[:, second_last.k, cols]
                             ).then_inc(stored[second_last.k], 16)
            sp.wait_ge(last_result_ready, 1)
            sp.dma_start(out_dram[last.at], as_rows(scaled[:, last.k])).then_inc(stored[last.k], 16)
            sp.wait_ge(stored[second_last.k], 16 * (second_last.half + T))
            sp.wait_ge(stored[last.k], 16 * (last.half + 1))

        @block.gpsimd
        def _(pool):
            nc.gpsimd.iota(stage_id[:, :], pattern=[[0, 1]], base=0, channel_multiplier=1,
                           allow_small_or_imprecise_dtypes=True).then_inc(ids_ready, 1)
            nc.gpsimd.memset(ident[:, :], 0.0).then_inc(ident_clear, 1)
            nc.gpsimd.memset(ident16[:, :], 0.0).then_inc(ident_clear, 1)
            pool.wait_ge(ident_clear, 2)
            for square in (ident, ident16):
                nc.gpsimd.affine_select(out=square[:, :], in_=square[:, :], compare_op=ALU.not_equal,
                                        fill=1.0, base=0, pattern=[[1, P]], channel_multiplier=-1
                                        ).then_inc(ident_ready, 1)
            nc.gpsimd.memset(ones[:, :], 1.0).then_inc(ones_ready, 1)
            pool.wait_ge(bias_ready, 1)
            pool.wait_ge(q_ready, 1)

            def step(batch):
                if b := batch(-1):
                    wait(pool, x_loaded[b.k], 16 * b.half + 16)
                    wait(pool, q_in_bank, b.at - 1)
                    nc.gpsimd.tensor_tensor(
                        q_nat[:, b.k], x_all[:, b.at].rearrange("p (t d) -> p t d", t=T),
                        bias[:, b.at].unsqueeze(2).broadcast_to([P, T, D]), ALU.add
                    ).then_inc(q_ready, 1)
                if b := batch(LAG_OUT):
                    wait(pool, scaled_ready, b.at + 1)
                    wait(pool, stored[b.k], 16 * b.half)
                    nc.gpsimd.tensor_tensor(
                        result[:, b.k], as_rows(scaled[:, b.k]),
                        x_all[:, b.at], ALU.add).then_inc(result_ready, 1)

            def weight_scales():
                pool.wait_ge(w_sums_ready, 1)
                nc.gpsimd.tensor_scalar(w_scale[:, :], w_sum[:, :], 1.0 / D, MIN_ABS,
                                        ALU.mult, ALU.max).then_inc(w_scale_ready, 1)
                pool.wait_ge(w_scale_ready, 1)
                nc.gpsimd.tensor_scalar(w_below[:, :], w_scale[:, :], -0.5, None, ALU.mult
                                        ).then_inc(w_bounds_ready, 1)
                nc.gpsimd.tensor_scalar(w_above[:, :], w_scale[:, :], 0.5, None, ALU.mult
                                        ).then_inc(w_bounds_ready, 1)

            def weight_signs():
                pool.wait_ge(weight_loaded, 16)
                pool.wait_ge(w_bounds_ready, 2)
                for t in range(T):
                    nc.gpsimd.tensor_scalar(w_neg[:, t], w_raw[:, t], w_below[:, t:t + 1], None,
                                            ALU.is_lt).then_inc(w_signs_ready, 1)
                    nc.gpsimd.tensor_scalar(w_pos[:, t], w_raw[:, t], w_above[:, t:t + 1], None,
                                            ALU.is_gt).then_inc(w_signs_ready, 1)
                pool.wait_ge(w_signs_ready, 2 * T)
                nc.gpsimd.tensor_tensor(tern[:, :, :], w_pos[:, :, :], w_neg[:, :, :], ALU.subtract
                                        ).then_inc(tern_ready, 1)

            for i in range(2 * LOOP_FROM):
                if i == 2:
                    weight_scales()
                if i == 3:
                    weight_signs()
                step(peeled(i))
            with pool.Fori(LOOP_FROM, B // 2 - 1) as half:
                for odd in range(2):
                    step(looped(half, odd))
            for i in range(B - 2, B + LAG_OUT - 3):
                step(peeled(i))
            third_last, second_last = Batch(0, B - 3), Batch(0, B - 2)
            pool.wait_ge(scaled_ready, third_last.at + 1)
            pool.wait_ge(row_ready, 1)
            nc.gpsimd.tensor_tensor(scaled[:, third_last.k], scaled[:, third_last.k],
                                    w_scale_row[:, :].unsqueeze(1).broadcast_to([P, T, O]), ALU.mult
                                    ).then_inc(columns_scaled, 1)
            pool.wait_ge(columns_scaled, 1)
            pool.wait_ge(stored[third_last.k], 16 * third_last.half)
            nc.gpsimd.tensor_tensor(
                result[:, third_last.k], as_rows(scaled[:, third_last.k]),
                x_all[:, third_last.at], ALU.add).then_inc(result_ready, 1)
            pool.wait_ge(stored[second_last.k], 16 * second_last.half)
            for t in range(T):
                pool.wait_ge(tiles_scaled, t + 1)
                cols = slice(t * D, (t + 1) * D)
                nc.gpsimd.tensor_tensor(result[:, second_last.k, cols], scaled[:, second_last.k, t],
                                        x_all[:, second_last.at, cols], ALU.add
                                        ).then_inc(tile_results_ready, 1)

        @block.tensor
        def _(pe):
            pe.wait_ge(warm_ready, 1)

            def keep_warm(products):
                for _ in range(products):
                    pe.matmul(out_bank[:, :, :], warm[:, 0:P], warm[:, :], start=True, stop=True)

            keep_warm(WARM)
            pe.wait_ge(ident_ready, 2)

            def bias_product():
                pe.wait_ge(one_hot_ready, 1)
                rows = embed_sb[:, :].rearrange("g (p t) -> g t p", t=T)
                for t in range(T):
                    mm = pe.matmul(score_bank[:, t, 0:B], rows[:, t], one_hot[:, :],
                                   start=True, stop=True)
                mm.then_inc(bias_in_bank, 1)

            def weights():
                pe.wait_ge(tern_ready, 1)
                for c in range(C):
                    for t in range(T):
                        pe.transpose(tern_half[:, c, t * P:(t + 1) * P],
                                     tern[:, t, c * P:(c + 1) * P], ident16[:, :])
                pe.wait_ge(diag_ready, 1)
                pe.wait_ge(ones_ready, 1)
                for t in range(T):
                    mm = pe.matmul(out_bank[:, 0, t * P:(t + 1) * P], ones[:, :], w_diag[:, t],
                                   start=True, stop=True)
                mm.then_inc(weights_in_bank, 1)

            def turn(to, of, by, tiles=range(T)):
                for c in range(C):
                    for t in tiles:
                        mm = pe.transpose(to[:, c, t * P:(t + 1) * P], of[:, t, c * P:(c + 1) * P], by)
                return mm

            def product(to, parts, tiles=range(T), wait_for_last_part=None):
                for t in tiles:
                    terms = [(left, right, c) for left, right in parts for c in range(C)]
                    for n, (left, right, c) in enumerate(terms):
                        if wait_for_last_part and t == tiles[0] and n == len(terms) - C:
                            wait_for_last_part()
                        mm = pe.matmul(to[:, t], left[:, c, t * P:(t + 1) * P], right[:, c],
                                       start=n == 0, stop=n == len(terms) - 1)
                return mm

            def turn_f(b):
                wait(pe, f_loaded[b.k], 16 * b.half + 16)
                wait(pe, f_lo_ready, b.at)
                turn(f_bank, f_nat[:, b.k], ident[:, :]).then_inc(f_in_bank, 1)

            def turn_q(b):
                wait(pe, q_ready, b.at + 1)
                wait(pe, q_lo_ready, b.at)
                turn(q_bank, q_nat[:, b.k], ident[:, :]).then_inc(q_in_bank, 1)

            def turn_prob(b):
                wait(pe, prob_ready, b.at + 1)
                wait(pe, prob_lo_ready, b.at)
                turn(prob_bank, prob, ident[:, :]).then_inc(prob_in_bank, 1)

            def score(b):
                wait(pe, f_lo_ready, b.at + 1)
                wait(pe, q_lo_ready, b.at + 1)
                wait(pe, prob_ready, b.at)
                product(score_bank, [(q_hi[:, b.k], f_hi[:, b.k]), (q_hi[:, b.k], f_lo[:, b.k]),
                                     (q_lo[:, b.k], f_hi[:, b.k])]).then_inc(score_in_bank, 1)

            def low_half_words(of):
                return of[:, :, :].bitcast(BF16).rearrange("p t (d h) -> p t d h", h=2)[:, :, :, 0]

            def turn_code(b):
                wait(pe, code_ready, b.at + 1)
                wait(pe, code_t_ready, b.at)
                turn(code_bank, low_half_words(code), ident16[:, :]).then_inc(code_in_bank, 1)

            def times_hadamard(b):
                wait(pe, f_lo_ready, b.at + 1)
                wait(pe, fh_lo_ready, b.at)
                product(fh_bank, [(f_hi[:, b.k], had), (f_lo[:, b.k], had)]).then_inc(fh_in_bank, 1)

            def mixed(b):
                return [(prob_hi[:, b.k], fh_hi[:, b.k]), (prob_hi[:, b.k], fh_lo[:, b.k]),
                        (prob_lo[:, b.k], fh_hi[:, b.k])]

            def mix(b):
                wait(pe, prob_lo_ready, b.at + 1)
                wait(pe, fh_lo_ready, b.at + 1)
                wait(pe, code_ready, b.at)
                product(xh_bank, mixed(b)).then_inc(xh_in_bank, 1)

            def times_ternary(b):
                wait(pe, code_t_ready, b.at + 1)
                wait(pe, scaled_ready, b.at)
                product(out_bank, [(code_t[:, b.k], tern_t)]).then_inc(out_in_bank, 1)

            STAGES_IN_ORDER = (
                (turn_f, LAG_LOAD_TURN), (turn_q, LAG_LOAD_TURN), (turn_prob, LAG_MIX),
                (score, LAG_SCORE), (turn_code, LAG_QUANT), (times_hadamard, LAG_SCORE),
                (mix, LAG_MIX), (times_ternary, LAG_QUANT))

            def step(batch):
                for stage, lag in STAGES_IN_ORDER:
                    if b := batch(lag):
                        stage(b)

            b0, b1, b2 = (Batch(0, n) for n in range(3))
            bias_product()
            turn_f(b0)
            keep_warm(1)
            turn_q(b0)
            keep_warm(1)
            turn_f(b1)
            pe.wait_ge(had_ready, 1)
            times_hadamard(b0)
            pe.wait_ge(bias_ready, 1)
            score(b0)
            turn_q(b1)
            turn_f(b2)
            times_hadamard(b1)
            turn_prob(b0)
            turn_q(b2)
            score(b1)
            mix(b0)
            for stage, lag in STAGES_IN_ORDER:
                if b := peeled(3)(lag):
                    if stage == times_hadamard:
                        weights()
                    if stage == times_ternary:
                        pe.wait_ge(tern_t_ready, 1)
                        pe.wait_ge(row_ready, 1)
                    stage(b)
            for i in range(4, 2 * LOOP_FROM):
                step(peeled(i))
            with pe.Fori(LOOP_FROM, B // 2) as half:
                for odd in range(2):
                    step(looped(half, odd))
            third_last, second_last, last = (Batch(0, B - n) for n in (3, 2, 1))
            score(last)
            turn_prob(second_last)
            turn_code(third_last)
            times_hadamard(last)
            times_ternary(third_last)
            turn_prob(last)
            mix(second_last)
            pe.wait_ge(prob_hi_ready, B)
            pe.wait_ge(fh_lo_ready, B)
            for t in range(T):
                product(last_xh_banks[t], mixed(last), [t],
                        wait_for_last_part=lambda: pe.wait_ge(prob_lo_ready, B)
                        ).then_inc(last_xh_in_bank, 1)
            turn_code(second_last)
            pe.wait_ge(code_ready, B - 1)
            for t in range(T):
                pe.wait_ge(last_code_ready, t + 1)
                turn(last_code_banks[t], low_half_words(last_code), ident16[:, :], [t]
                     ).then_inc(last_code_in_bank, 1)
                if t == 0:
                    pe.wait_ge(code_t_ready, B - 1)
                    pe.wait_ge(scaled_ready, B - 2)
                    for u in range(T):
                        product(second_last_out_banks[u], [(code_t[:, second_last.k], tern_t)], [u]
                                ).then_inc(tiles_out_in_bank, 1)
            for t in range(T):
                pe.wait_ge(last_code_t_ready, t + 1)
                product(last_out_banks[t], [(code_t[:, last.k], tern_t)], [t]
                        ).then_inc(tiles_out_in_bank, 1)

        @block.scalar
        def _(act):
            act.dma_start(stage_of[:, :], itok.partition_broadcast(STAGES)).then_inc(bias_loaded, 16)
            act.wait_ge(warm_ready, 1)
            nc.scalar.activation(row_sum[:, 0], warm[:, 0:T], ACT.Exp)

            def split_f(b):
                wait(act, fh_in_bank, b.at - 1)
                wait(act, f_in_bank, b.at + 1)
                nc.scalar.copy(f_hi[:, b.k], f_bank[:, :, :]).then_inc(f_hi_ready, 1)

            def split_q(b):
                wait(act, q_in_bank, b.at + 1)
                nc.scalar.copy(q_hi[:, b.k], q_bank[:, :, :]).then_inc(q_hi_ready, 1)

            def quantize_tile(to, xh, t, b):
                return nc.scalar.activation(to[:, t], xh[:, t], ACT.Copy, bias=MAGIC,
                                            scale=inv_scale[:, b.k, t:t + 1])

            def quantize(b):
                wait(act, inv_scale_ready, b.at + 1)
                for t in range(T):
                    a = quantize_tile(code, xh_bank, t, b)
                a.then_inc(code_ready, 1)

            def split_prob(b):
                wait(act, prob_in_bank, b.at + 1)
                nc.scalar.copy(prob_hi[:, b.k], prob_bank[:, :, :]).then_inc(prob_hi_ready, 1)

            def decode(b):
                wait(act, code_in_bank, b.at + 1)
                nc.scalar.activation(code_t[:, b.k], code_bank[:, 0:C], ACT.Copy,
                                     bias=-CODE_ONE * CODE_STEP, scale=CODE_STEP
                                     ).then_inc(code_t_ready, 1)

            def split_fh(b):
                wait(act, fh_in_bank, b.at + 1)
                nc.scalar.copy(fh_hi[:, b.k], fh_bank[:, :, :]).then_inc(fh_hi_ready, 1)

            def exponentials(b):
                wait(act, neg_max_ready, b.at + 1)
                for t in range(T):
                    a = nc.scalar.activation(prob[:, t], score_bank[:, t], ACT.Exp,
                                             bias=neg_max[:, b.k, t:t + 1],
                                             accum_out=row_sum[:, b.k, t:t + 1])
                a.then_inc(prob_ready, 1)

            STAGES_IN_ORDER = (
                (split_f, LAG_LOAD_TURN), (split_q, LAG_LOAD_TURN), (quantize, LAG_QUANT),
                (split_prob, LAG_MIX), (decode, LAG_QUANT), (split_fh, LAG_SCORE),
                (exponentials, LAG_SCORE))

            def step(batch):
                for stage, lag in STAGES_IN_ORDER:
                    if b := batch(lag):
                        stage(b)

            b0, b1, b2, b3 = (Batch(0, n) for n in range(4))
            split_f(b0)
            split_q(b0)
            split_f(b1)
            split_fh(b0)
            act.wait_ge(weight_loaded, 16)
            for t in range(T):
                a = nc.scalar.activation(w_abs[:, t], w_raw[:, t], ACT.Abs,
                                         accum_out=w_sum[:, t:t + 1])
            a.then_inc(w_sums_ready, 1)
            split_q(b1)
            exponentials(b0)
            split_f(b2)
            split_prob(b0)
            split_fh(b1)
            split_q(b2)
            act.wait_ge(w_scale_ready, 1)
            for t in range(T):
                a = nc.scalar.activation(w_diag[:, t], ident[:, :], ACT.Copy, scale=w_scale[:, t:t + 1])
            a.then_inc(diag_ready, 1)
            exponentials(b1)
            split_f(b3)
            quantize(b0)
            split_q(b3)
            split_prob(b1)
            decode(b0)
            split_fh(b2)
            exponentials(b2)
            for i in range(4, 2 * LOOP_FROM):
                step(peeled(i))
            with act.Fori(LOOP_FROM, B // 2) as half:
                for odd in range(2):
                    step(looped(half, odd))
            third_last, second_last, last = (Batch(0, B - n) for n in (3, 2, 1))
            quantize(third_last)
            split_prob(second_last)
            exponentials(last)
            split_fh(last)
            split_prob(last)
            act.wait_ge(out_in_bank, third_last.at + 1)
            act.wait_ge(out_scale_ready, third_last.at + 1)
            act.wait_ge(result_ready, third_last.at - 1)
            for t in range(T):
                a = nc.scalar.activation(scaled[:, third_last.k, t], out_bank[:, t], ACT.Copy,
                                         scale=out_scale[:, third_last.k, t:t + 1])
            a.then_inc(scaled_ready, 1)
            quantize(second_last)
            act.wait_ge(inv_scale_ready, B)
            for t in range(T):
                quantize_tile(last_code, last_xh_banks[t], t, last).then_inc(last_code_ready, 1)
            for t in range(T):
                act.wait_ge(last_code_in_bank, t + 1)
                rows = slice(t * P, (t + 1) * P)
                nc.scalar.activation(code_t[:, last.k, :, rows], last_code_banks[t][:, 0:C, rows],
                                     ACT.Copy, bias=-CODE_ONE * CODE_STEP, scale=CODE_STEP
                                     ).then_inc(last_code_t_ready, 1)

        @block.vector
        def _(dve):
            nc.vector.memset(warm[:, :], 0.0).then_inc(warm_ready, 1)
            dve.wait_ge(bias_loaded, 32)
            dve.wait_ge(ids_ready, 1)
            nc.vector.tensor_scalar(one_hot[:, :], stage_of[:, :], stage_id[:, 0:1], None,
                                    ALU.is_equal).then_inc(one_hot_ready, 1)
            dve.wait_ge(bias_in_bank, 1)
            nc.vector.tensor_copy(bias[:, :, :].rearrange("p b t -> p t b"),
                                  score_bank[:, :, 0:B]).then_inc(bias_ready, 1)

            def weight_copies():
                dve.wait_ge(weights_in_bank, 1)
                nc.vector.tensor_copy(tern_t[:, :, :], tern_half).then_inc(tern_t_ready, 1)
                nc.vector.tensor_copy(w_scale_row[:, :], out_bank[:, 0]).then_inc(row_ready, 1)

            def scales(b):
                wait(dve, xh_in_bank, b.at + 1)
                nc.vector.tensor_reduce(abs_max[:, :], xh_bank[:, :, :], AX.X, ALU.max,
                                        apply_absolute_value=True).then_inc(abs_max_ready, 1)
                wait(dve, abs_max_ready, b.at + 1)
                row_scales(b, out_scale[:, b.k])

            def row_scales(b, to_out):
                wait(dve, sums_ready, 2 * b.at + 2)
                nc.vector.scalar_tensor_tensor(
                    out=raw_scale[:, :], in0=abs_max[:, :], scalar=1.0 / POS,
                    in1=least_scale[:, b.k], op0=ALU.mult, op1=ALU.max
                ).then_inc(raw_scale_ready, 1)
                wait(dve, raw_scale_ready, b.at + 1)
                nc.vector.reciprocal(inv_scale[:, b.k], raw_scale[:, :]).then_inc(inv_scale_ready, 1)
                nc.vector.tensor_tensor(to_out, raw_scale[:, :], inv_sum[:, b.k], ALU.mult
                                        ).then_inc(out_scale_ready, 1)

            def scale_tile(product, t, b, scale):
                return nc.vector.scalar_tensor_tensor(
                    out=scaled[:, b.k, t], in0=product[:, t], scalar=scale[:, t:t + 1],
                    in1=w_scale_row[:, :], op0=ALU.mult, op1=ALU.mult)

            def scale_out(b):
                wait(dve, out_in_bank, b.at + 1)
                wait(dve, out_scale_ready, b.at + 1)
                wait(dve, result_ready, b.at - 1)
                for t in range(T):
                    v = scale_tile(out_bank, t, b, out_scale[:, b.k])
                v.then_inc(scaled_ready, 1)

            def low_part(low, of, high):
                return nc.vector.tensor_tensor(low, of[:, :, :], high.bitcast(F32), ALU.subtract)

            def split_f(b):
                wait(dve, f_hi_ready, b.at + 1)
                low_part(f_lo[:, b.k], f_bank, f_hi[:, b.k]).then_inc(f_lo_ready, 1)

            def split_q(b):
                wait(dve, q_hi_ready, b.at + 1)
                low_part(q_lo[:, b.k], q_bank, q_hi[:, b.k]).then_inc(q_lo_ready, 1)

            def split_prob(b):
                wait(dve, prob_hi_ready, b.at + 1)
                low_part(prob_lo[:, b.k], prob_bank, prob_hi[:, b.k]).then_inc(prob_lo_ready, 1)

            def split_fh(b):
                wait(dve, fh_hi_ready, b.at + 1)
                low_part(fh_lo[:, b.k], fh_bank, fh_hi[:, b.k]).then_inc(fh_lo_ready, 1)

            def sums(b):
                wait(dve, prob_ready, b.at + 1)
                nc.vector.reciprocal(inv_sum[:, b.k], row_sum[:, b.k]).then_inc(sums_ready, 1)
                nc.vector.tensor_scalar(least_scale[:, b.k], row_sum[:, b.k], MIN_ABS / POS, None,
                                        ALU.mult).then_inc(sums_ready, 1)

            def maximum(b):
                wait(dve, score_in_bank, b.at + 1)
                nc.vector.tensor_reduce(neg_max[:, b.k], score_bank[:, :, :], AX.X, ALU.max,
                                        negate=True).then_inc(neg_max_ready, 1)

            def decode(b):
                dve.wait_ge(code_in_bank, b.at + 1)
                nc.vector.tensor_scalar(code_t[:, b.k], code_bank[:, 0:C], CODE_STEP,
                                        -CODE_ONE * CODE_STEP, ALU.mult, ALU.add
                                        ).then_inc(code_t_ready, 1)

            STAGES_IN_ORDER = (
                (scales, LAG_QUANT), (scale_out, LAG_OUT), (split_f, LAG_LOAD_TURN),
                (split_q, LAG_LOAD_TURN), (split_prob, LAG_MIX), (sums, LAG_MIX),
                (maximum, LAG_SCORE), (split_fh, LAG_SCORE))

            def step(batch):
                for stage, lag in STAGES_IN_ORDER:
                    if b := batch(lag):
                        stage(b)

            dve.wait_ge(x_loaded[0], 16)
            dve.wait_ge(bias_ready, 1)
            nc.vector.tensor_tensor(
                q_nat[:, 0], x_all[:, 0].rearrange("p (t d) -> p t d", t=T),
                bias[:, 0].unsqueeze(2).broadcast_to([P, T, D]), ALU.add).then_inc(q_ready, 1)
            b0, b1, b2 = (Batch(0, n) for n in range(3))
            dve.wait_ge(had_loaded, 16)
            nc.vector.tensor_copy(had[:, :, :], had_raw[:, :, :]).then_inc(had_ready, 1)
            split_f(b0)
            split_q(b0)
            split_f(b1)
            split_fh(b0)
            maximum(b0)
            split_q(b1)
            split_f(b2)
            split_prob(b0)
            split_fh(b1)
            sums(b0)
            maximum(b1)
            split_q(b2)
            for stage, lag in STAGES_IN_ORDER:
                if b := peeled(3)(lag):
                    if stage == split_fh:
                        weight_copies()
                    stage(b)
            for i in range(4, 2 * LOOP_FROM):
                step(peeled(i))
            with dve.Fori(LOOP_FROM, B // 2) as half:
                for odd in range(2):
                    step(looped(half, odd))
            fourth_last, third_last, second_last, last = (Batch(0, B - n) for n in (4, 3, 2, 1))
            scales(third_last)
            scale_out(fourth_last)
            maximum(last)
            decode(third_last)
            split_prob(second_last)
            sums(second_last)
            sums(last)
            split_fh(last)
            split_prob(last)
            scales(second_last)
            for t in range(T):
                dve.wait_ge(last_xh_in_bank, t + 1)
                nc.vector.tensor_reduce(abs_max[:, t:t + 1], last_xh_banks[t][:, t], AX.X, ALU.max,
                                        apply_absolute_value=True).then_inc(last_abs_ready, 1)
            dve.wait_ge(last_abs_ready, T)
            row_scales(last, last_out_scale[:, :])
            decode(second_last)
            dve.wait_ge(result_ready, second_last.at - 1)
            for t in range(T):
                dve.wait_ge(tiles_out_in_bank, t + 1)
                scale_tile(second_last_out_banks[t], t, second_last,
                           out_scale[:, second_last.k]).then_inc(tiles_scaled, 1)
            dve.wait_ge(out_scale_ready, B)
            dve.wait_ge(result_ready, B - 2)
            for t in range(T):
                dve.wait_ge(tiles_out_in_bank, T + t + 1)
                scale_tile(last_out_banks[t], t, last, last_out_scale).then_inc(tiles_scaled, 1)
            dve.wait_ge(tiles_scaled, 2 * T)
            nc.vector.tensor_tensor(as_rows(scaled[:, last.k]), as_rows(scaled[:, last.k]),
                                    x_all[:, last.at], ALU.add).then_inc(last_result_ready, 1)


def hadamard_matrix(size):
    h = np.ones((1, 1))
    while len(h) < size:
        h = np.block([[h, h], [h, -h]])
    return (h / np.sqrt(size)).astype(np.float32)


def kernel(x, fside_BxSxS_0, itok_B_0_5, L0_cond_braak_embed, L0_ffn_weight):
    import concourse.bacc as bacc
    from concourse.bass_utils import run_bass_kernel_spmd

    nc = bacc.Bacc("TRN2", target_bir_lowering=False, num_devices=1)
    arrays = {
        "x": x,
        "f": fside_BxSxS_0,
        "itok": itok_B_0_5,
        "embed": L0_cond_braak_embed,
        "weight": L0_ffn_weight,
        "hadamard": hadamard_matrix(x.shape[-1]),
    }
    arrays = {f"{name}_dram": np.ascontiguousarray(a) for name, a in arrays.items()}
    ins = [nc.dram_tensor(name, a.shape, mybir.dt.from_np(a.dtype), kind="ExternalInput").ap()
           for name, a in arrays.items()]
    out = nc.dram_tensor("out_dram", x.shape, F32, kind="ExternalOutput").ap()
    adaln_ffn_kernel(nc, *ins, out)
    results = run_bass_kernel_spmd(nc, [arrays], core_ids=[0]).results
    return results[0]["out_dram"]
```
